# Optimizing a Trainium2 kernel written in Bass

```python
import numpy as np
import jax
import jax.numpy as jnp

def _softmax(x, axis=-1):
    return jax.nn.softmax(x, axis=axis)

def _gelu(x):
    return jax.nn.gelu(x, approximate=True)

def _silu(x):
    return jax.nn.silu(x)

def _sigmoid(x):
    return jax.nn.sigmoid(x)

def _layernorm(x, axis=-1, eps=1e-05):
    m = jnp.mean(x, axis=axis, keepdims=True)
    v = jnp.var(x, axis=axis, keepdims=True)
    return (x - m) / jnp.sqrt(v + eps)

def _scatter_add(tgt, idx, src, axis=0):
    return tgt.at[idx].add(src)

def _segment_sum(src, seg, n):
    return jax.ops.segment_sum(src, seg, n)
kernel_name = 'mk_xattn_ffn_d1_seqx_r4_ee46e8'

def setup_inputs(seed: int=0):
    np.random.seed(seed)
    _w = jnp.asarray

    def _rec_inputs():
        import jax
        import jax.numpy as jnp
        _rk = jax.random.key(seed)
        x = -0.0003929 + 0.9999 * jax.random.normal(jax.random.fold_in(_rk, 1), (16, 512, 256), jnp.float32)
        _lenS = 512 - jax.random.randint(jax.random.fold_in(_rk, 7), (16,), 0, max(1, 512 // 4) + 1, jnp.int32)
        _lenS2 = 1601 - jax.random.randint(jax.random.fold_in(_rk, 8), (16,), 0, max(1, 1601 // 4) + 1, jnp.int32)
        _ctx_512P = jax.random.normal(jax.random.fold_in(_rk, 11), (16, 16, 128), jnp.float32)
        _ctx_512c = jax.random.dirichlet(jax.random.fold_in(_rk, 511), 0.3 * jnp.ones((16,), jnp.float32), (16, 1601))
        _ctx_512t = jnp.einsum('bsk,bkd->bsd', _ctx_512c, _ctx_512P)
        _ctx_512t = _ctx_512t * jax.lax.rsqrt(jnp.mean(jnp.square(_ctx_512t)) + 1e-12) * 0.953939
        ctx_512 = -1.39393e-06 + 0.999914 * (_ctx_512t + 0.3 * jax.random.normal(jax.random.fold_in(_rk, 611), (16, 1601, 128), jnp.float32))
        return (x, ctx_512)
    x, ctx_512 = _rec_inputs()

    def _L0_xattn_setup():
        import jax, jax.numpy as jnp
        import numpy as np
        HEADS = 16
        D_MODEL = 256
        IMG_MODEL = 128
        D_K = D_MODEL // HEADS
        key = jax.random.key(seed)
        ks = jax.random.split(key, 12)
        B, LQ, LKV = (8, 512, 256)
        s_dm = 1.0 / np.sqrt(D_MODEL)
        s_im = 1.0 / np.sqrt(IMG_MODEL)
        return {'q': jax.random.normal(ks[0], (B, LQ, D_MODEL), jnp.float32), 'k': jax.random.normal(ks[1], (B, LKV, IMG_MODEL), jnp.float32), 'v': jax.random.normal(ks[2], (B, LKV, IMG_MODEL), jnp.float32), 'Wq': jax.random.normal(ks[3], (D_MODEL, D_MODEL), jnp.float32) * s_dm, 'bq': jnp.zeros((D_MODEL,), jnp.float32), 'Wk': jax.random.normal(ks[4], (IMG_MODEL, D_MODEL), jnp.float32) * s_im, 'bk': jnp.zeros((D_MODEL,), jnp.float32), 'Wv': jax.random.normal(ks[5], (IMG_MODEL, D_MODEL), jnp.float32) * s_im, 'bv': jnp.zeros((D_MODEL,), jnp.float32), 'Wo': jax.random.normal(ks[6], (D_MODEL, D_MODEL), jnp.float32) * s_dm, 'bo': jnp.zeros((D_MODEL,), jnp.float32)}
    _L0_xattn_all = _L0_xattn_setup()
    _L0_xattn_in = {k: v for k, v in _L0_xattn_all.items() if k in ('Wq', 'bq', 'Wk', 'bk', 'Wv', 'bv', 'Wo', 'bo')}
    del _L0_xattn_all

    def _L0_ffn_setup():
        import jax, jax.numpy as jnp
        import numpy as np
        N_EMBD = 256
        N_EXP = 8
        TOP_K = 2
        CAPACITY = 1024
        D_FF = 3 * N_EMBD
        key = jax.random.key(seed)
        k1, k2, k3, k4 = jax.random.split(key, 4)
        x = jax.random.normal(k1, (8, 512, N_EMBD), dtype=jnp.float32)
        w_gate = jax.random.normal(k2, (N_EMBD, N_EXP), dtype=jnp.float32) * 0.02
        c_fc = jax.random.normal(k3, (N_EXP, N_EMBD, D_FF), dtype=jnp.float32) * 0.02
        c_proj = jax.random.normal(k4, (N_EXP, D_FF // 2, N_EMBD), dtype=jnp.float32) * 0.02
        return {'x': x, 'w_gate': w_gate, 'c_fc': c_fc, 'c_proj': c_proj}
    _L0_ffn_all = _L0_ffn_setup()
    _L0_ffn_in = {k: v for k, v in _L0_ffn_all.items() if k in ('w_gate', 'c_fc', 'c_proj')}
    del _L0_ffn_all
    return {'x': x, 'ctx_512': ctx_512, 'L0_xattn_Wq': _L0_xattn_in['Wq'], 'L0_xattn_bq': _L0_xattn_in['bq'], 'L0_xattn_Wk': _L0_xattn_in['Wk'], 'L0_xattn_bk': _L0_xattn_in['bk'], 'L0_xattn_Wv': _L0_xattn_in['Wv'], 'L0_xattn_bv': _L0_xattn_in['bv'], 'L0_xattn_Wo': _L0_xattn_in['Wo'], 'L0_xattn_bo': _L0_xattn_in['bo'], 'L0_ffn_w_gate': _L0_ffn_in['w_gate'], 'L0_ffn_c_fc': _L0_ffn_in['c_fc'], 'L0_ffn_c_proj': _L0_ffn_in['c_proj']}

def reference(x, ctx_512, L0_xattn_Wq, L0_xattn_bq, L0_xattn_Wk, L0_xattn_bk, L0_xattn_Wv, L0_xattn_bv, L0_xattn_Wo, L0_xattn_bo, L0_ffn_w_gate, L0_ffn_c_fc, L0_ffn_c_proj):
    import jax
    import jax.numpy as jnp

    def _L0_xattn_ref(q, k, v, Wq, bq, Wk, bk, Wv, bv, Wo, bo):
        import jax, jax.numpy as jnp
        import numpy as np
        HEADS = 16
        D_MODEL = 256
        IMG_MODEL = 128
        D_K = D_MODEL // HEADS
        B, LQ, _ = q.shape
        LKV = k.shape[1]
        qh = (q @ Wq + bq).reshape(B, LQ, HEADS, D_K).transpose(0, 2, 1, 3)
        kh = (k @ Wk + bk).reshape(B, LKV, HEADS, D_K).transpose(0, 2, 1, 3)
        vh = (v @ Wv + bv).reshape(B, LKV, HEADS, D_K).transpose(0, 2, 1, 3)
        scale = 1.0 / np.sqrt(D_K)
        scores = jnp.einsum('bhqd,bhkd->bhqk', qh, kh) * scale
        attn = jax.nn.softmax(scores, axis=-1)
        out = jnp.einsum('bhqk,bhkd->bhqd', attn, vh)
        concat = out.transpose(0, 2, 1, 3).reshape(B, LQ, D_MODEL)
        return concat @ Wo + bo

    def _L0_ffn_ref(x, w_gate, c_fc, c_proj):
        import jax, jax.numpy as jnp
        import numpy as np
        N_EMBD = 256
        N_EXP = 8
        TOP_K = 2
        CAPACITY = 1024
        D_FF = 3 * N_EMBD
        B, T, d = x.shape
        N = B * T
        xf = x.reshape(N, d)
        scores = jax.nn.softmax(xf @ w_gate, axis=-1)
        weights, idx = jax.lax.top_k(scores, TOP_K)
        flat_e = idx.reshape(-1)
        tok = jnp.repeat(jnp.arange(N), TOP_K)
        oh = jax.nn.one_hot(flat_e, N_EXP, dtype=jnp.int32)
        pos = (jnp.cumsum(oh, axis=0) * oh).sum(-1) - 1
        valid = pos < CAPACITY
        pos_c = jnp.where(valid, pos, 0)
        vmask = valid.astype(x.dtype)[:, None]
        exp_x = jnp.zeros((N_EXP, CAPACITY, d), x.dtype)
        exp_x = exp_x.at[flat_e, pos_c].add(xf[tok] * vmask)
        h = jnp.einsum('ecd,edf->ecf', exp_x, c_fc)
        a, g = jnp.split(h, 2, axis=-1)
        h = jax.nn.silu(a) * g
        exp_out = jnp.einsum('ecf,efd->ecd', h, c_proj)
        gathered = exp_out[flat_e, pos_c]
        w = weights.reshape(-1)[:, None] * vmask
        out = (gathered * w).reshape(N, TOP_K, d).sum(axis=1)
        return out.reshape(B, T, d)
    x = x + _L0_xattn_ref(_layernorm(x, axis=-1), ctx_512, ctx_512, L0_xattn_Wq, L0_xattn_bq, L0_xattn_Wk, L0_xattn_bk, L0_xattn_Wv, L0_xattn_bv, L0_xattn_Wo, L0_xattn_bo)
    x = x + _L0_ffn_ref(_layernorm(x, axis=-1), L0_ffn_w_gate, L0_ffn_c_fc, L0_ffn_c_proj)
    return x

_drawn_inputs = setup_inputs


def setup_inputs(seed=0):
    import zlib

    import numpy as np

    out = dict(_drawn_inputs(seed))
    spreads = {'L0_xattn_bq': (0.0, 0.404),
     'L0_xattn_bk': (0.0, 0.8),
     'L0_xattn_bv': (0.0, 0.1),
     'L0_xattn_bo': (0.0, 0.1)}
    factors = {'L0_ffn_w_gate': 8.0, 'L0_ffn_c_fc': 8.0, 'L0_ffn_c_proj': 8.0}
    for name, (base, spread) in spreads.items():
        noise = np.random.default_rng([zlib.crc32(name.encode()), seed]).standard_normal(out[name].shape)
        drawn = base * np.exp(spread * noise) if base else spread * noise
        out[name] = jnp.asarray(drawn.astype(out[name].dtype))
    for name, factor in factors.items():
        out[name] = (out[name] * factor).astype(out[name].dtype)
    return out
```

```python
import concourse.bass as bass
from concourse import mybir
from contextlib import ExitStack

P = 128
ALU = mybir.AluOpType
ACT = mybir.ActivationFunctionType
AX = mybir.AxisListType
F32 = mybir.dt.float32
F32R = mybir.dt.float32r
BF16 = mybir.dt.bfloat16
I32 = mybir.dt.int32
U32 = mybir.dt.uint32

EPS = 1e-5
DH = 16
HG = 4
CAPACITY = 1024
SUM_REACH = 1e15
OUT_REACH = 1e30
MM = 512


def r(ap):
    return ap.bitcast(F32R)


def stand(eng, passed):
    eng.sem_inc(passed, 1)


def build(nc, x, ctx, Wq, bq, Wk, bk, Wv, bv, Wo, bo, w_gate, c_fc, c_proj, out):
    B, LQ, D = x.shape
    _, LK, DC = ctx.shape
    H = D // DH
    G = H // HG
    NQ = LQ // P
    ND = D // P
    NT = (LK + P - 1) // P
    LAST = LK - (NT - 1) * P
    NE = w_gate.shape[1]
    NTOK = B * LQ
    NTT = NTOK // P
    FF = c_fc.shape[2] // 2
    NF = FF // P
    XW = D + NE
    SCALE = float(DH) ** -0.5
    STEPS = G * NT
    NB32 = LQ // 32
    NKC = (LK + MM - 1) // MM

    xn2_dram = nc.dram_tensor("xn2_rows", (NTOK, XW), F32, kind="Internal").ap()
    out_rows = out.rearrange("b q d -> (b q) d")

    PREP = ([("xT", c) for c in range(ND)] + [("Q", c) for c in range(ND)]
            + [("cT", k) for k in range(NKC)]
            + [("K", c, n) for c in range(ND) for n in range(NKC)]
            + [("V", k) for k in range((NT + 1) // 2)])
    EPI = [("O", k) for k in range(NQ // 2)] + [("nT", c) for c in range(ND)] + [("lg",)]
    NP, NEP = len(PREP), len(EPI)
    xT_k, Q_k = PREP.index(("xT", 0)), PREP.index(("Q", 0))
    cT_k, K_k, V_k = PREP.index(("cT", 0)), PREP.index(("K", 0, 0)), PREP.index(("V", 0))
    O_k, nT_k, lg_k = EPI.index(("O", 0)), EPI.index(("nT", 0)), EPI.index(("lg",))

    late = {4: O_k, 6: O_k + 1, 11: nT_k, 12: nT_k + 1, 13: lg_k}
    prep_at = {}
    u = 18
    for k in range(NP):
        prep_at[u] = k
        u += 1
    assert u <= STEPS
    LN1_STATS, LN1_APPLY, GATE_EXP, GATE_END = 15, 17, 16, 17
    LINKS = 32

    with ExitStack() as es:
        def sb(name, shape, dt=F32):
            return es.enter_context(nc.sbuf_tensor(name, shape, dt))

        def sem(name):
            return es.enter_context(nc.semaphore(name))

        ident = sb("ident", [P, P])
        tri = sb("tri", [P, P], BF16)
        ones_b = sb("ones_b", [P, P], BF16)
        iota8 = sb("iota8", [P, NQ, NE])
        half = sb("half", [P, NQ])
        redo = sb("redo", [1, 1], I32)
        s_redo = sem("first_pass_judged")
        onehot = sb("onehot", [P, 2, NTT, NE], BF16)

        def attention(shifted):
            again = "_shifted" if shifted else ""
            with ExitStack() as es1:
                def sb1(name, shape, dt=F32):
                    return es1.enter_context(nc.sbuf_tensor(name + again, shape, dt))

                def sem1(name):
                    return es1.enter_context(nc.semaphore(name + again))

                sc = es1.enter_context(nc.psum_tensor("scores" + again, [P, 3, 2 * MM], F32))
                po = es1.enter_context(nc.psum_tensor("attn_out" + again, [P, MM], F32))
                pm = es1.enter_context(nc.psum_tensor("spare" + again, [P, MM], F32))
                wq = sb1("wq", [P, ND, D])
                wk = sb1("wk", [P, D])
                wv = sb1("wv", [P, D])
                wo = sb1("wo", [P, G // 2, D])
                wg = sb1("wg", [P, ND, NE])
                bqc = sb1("bqc", [P, ND])
                bkc = sb1("bkc", [P, ND])
                bvb = sb1("bvb", [P, D])
                bob = sb1("bob", [P, D])
                x_sb = sb1("x_sb", [P, NQ, D])
                xT = sb1("xT", [P, ND, LQ])
                cT = sb1("cT", [P, LK])
                q_hl = sb1("q_hl", [P, 2, ND, LQ])
                k_hl = sb1("k_hl", [P, 2, ND, LK + 1])
                q_st = sb1("q_st", [P, H, LQ])
                k_st = sb1("k_st", [P, H // 2, LK + 1])
                v_raw = sb1("v_raw", [P, NT, D])
                c_sb = v_raw[:, 0:(NT * DC + D - 1) // D, :].rearrange("p t d -> p (t d)")[:, 0:NT * DC].rearrange(
                    "p (t d) -> p t d", d=DC)
                VW = DH + 1
                v_st = sb1("v_st", [P, NT, H * VW + DH])
                pr = sb1("probs", [P, 2, 2, 2 * MM])
                o_t = sb1("o_t", [P, NB32, 32])
                o_n = sb1("o_n", [P, NB32, 32])
                rec = sb1("rec", [P, NB32])
                rok = sb1("rok", [P, NB32])
                at = sb1("attnT", [P, G // 2, LQ])
                x1 = sb1("x1", [P, NQ, D])
                xn2 = sb1("xn2", [P, NQ, XW])
                nT = xT
                st1 = sb1("st1", [P, NQ, 6])
                mv1 = sb1("mv1", [P, NQ, 2])
                rstd1 = sb1("rstd1", [P, NQ])
                st2 = sb1("st2", [P, NQ, 6])
                mv2 = sb1("mv2", [P, NQ, 2])
                rstd2 = sb1("rstd2", [P, NQ])
                lg = sb1("lg", [P, NQ, NE])
                mx = sb1("mx", [P, NQ, NE])
                mi = sb1("mi", [P, NQ, NE], U32)
                mif = sb1("mif", [P, NQ, 2])
                zz = sb1("zz", [P, NQ, NE])
                ez = sb1("ez", [P, NQ, NE])
                gs = sb1("gs", [P, NQ])
                oh = sb1("oh", [P, 2, NQ, NE])
                if shifted:
                    KM = HG * NQ
                    zrow = sb1("zrow", [2, LQ])
                    mxv = sb1("mxv", [P, KM])
                    mrow = sb1("mrow", [KM, 2, P])
                    s_mr = sem1("unshifted_scores_ready")
                    s_md = sem1("maxima_taken")
                    s_ms = sem1("shift_rows_filled")
                    sflat = sc[:, :, :].rearrange("p a b -> p (a b)")
                else:
                    red = sb1("red", [P, 2, B * G])
                    okc = sb1("okc", [P, 1])
                    onec = sb1("onec", [P, 1])

                s_const = sem1("consts_made")
                s_w = sem1("weights_loaded")
                s_x = sem1("x_loaded")
                s_c = sem1("ctx_loaded")
                s_xr = sem1("residual_loaded")
                s_st = [sem1(f"stacks_filled{g}") for g in range(G)]
                s_sc = sem1("scores_ready")
                s_exp = sem1("probs_ready")
                s_pv = sem1("pv_done")
                s_oc = sem1("attn_out_copied")
                s_prep = sem1("prep_item_ready")
                s_prepd = sem1("prep_item_taken")
                s_epi = sem1("epi_item_ready")
                s_epid = sem1("epi_item_taken")
                s_v = sem1("v_group_placed")
                s_mv1 = sem1("ln1_stats_ready")
                s_r1 = sem1("ln1_rstd_ready")
                s_mv2 = sem1("ln2_stats_ready")
                s_r2 = sem1("ln2_rstd_ready")
                s_bo = sem1("residual_biased")
                s_z = sem1("gate_logits_shifted")
                s_ez = sem1("gate_exp_ready")
                s_n = sem1("ln2_rows_ready")
                s_nx = sem1("routed_rows_ready")
                s_at = sem1("attnT_ready")
                s_xn = sem1("ln1_rows_ready")
                s_x1o = sem1("x1_stored")
                s_xno = sem1("routed_rows_stored")
                s_ok = sem1("verdict_per_partition")
                s_okp = sem1("verdict_summed")
                s_past = sem1("dve_waits_passed")
                s_past_p = sem1("pool_waits_passed")
                s_dve = sem1("dve_step")

                block = es1.enter_context(nc.Block())

                def program(engine):
                    def declare(steps):
                        @engine
                        def _(eng):
                            if not shifted:
                                steps(eng)
                            else:
                                eng.wait_ge(s_redo, 1)
                                with eng.If(eng.value_load(redo[0:1, 0:1], min_val=0, max_val=P)):
                                    steps(eng)
                    return declare

                NCONST = 13
                NW = 16 * (2 + 1 + 1 + 2 * HG + 1 + 2 + 2)

                STK = 16 * HG * (7 if shifted else 6)

                @program(block.sync)
                def _(sp):
                    sp.dma_start(x_sb[:, :, :], x[0].rearrange("(t p) d -> p t d", p=P)).then_inc(s_x, 16)
                    for c in range(ND):
                        sp.dma_start(wq[:, c, :], Wq[c * P:(c + 1) * P, :]).then_inc(s_w, 16)
                    sp.wait_ge(s_const, NCONST)
                    sp.dma_start(c_sb[:, 0:NT - 1, :],
                                 ctx[0, 0:(NT - 1) * P].rearrange("(t p) d -> p t d", p=P)).then_inc(s_c, 16)
                    sp.dma_start(c_sb[0:LAST, NT - 1, :], ctx[0, (NT - 1) * P:LK]).then_inc(s_c, 16)
                    sp.dma_start(wk[:, :], Wk).then_inc(s_w, 16)
                    sp.dma_start(wv[:, :], Wv).then_inc(s_w, 16)
                    with nc.allow_non_contiguous_dma(reason="bias columns and gate weights, once"):
                        sp.dma_start(bqc[:, :], bq.rearrange("(c p) -> p c", p=P)).then_inc(s_w, 16)
                        sp.dma_start(bkc[:, :], bk.rearrange("(c p) -> p c", p=P)).then_inc(s_w, 16)
                    sp.dma_start(wg[:, :, :], w_gate.rearrange("(c p) e -> p c e", p=P)).then_inc(s_w, 16)
                    sp.dma_start(bvb[:, :], bv.rearrange("(a n) -> a n", a=1).broadcast_to([P, D])).then_inc(s_w, 16)
                    sp.dma_start(bob[:, :], bo.rearrange("(a n) -> a n", a=1).broadcast_to([P, D])).then_inc(s_w, 16)
                    wo_v = Wo.rearrange("(p i h d) n -> h i d p n", i=2, h=HG, d=DH)
                    for h in range(HG):
                        for i in range(2):
                            row = 32 * h + DH * i
                            sp.dma_start(wo[row:row + DH, :, :], wo_v[h, i]).then_inc(s_w, 16)

                    def stacks(b, g):
                        if not (isinstance(b, int) and b == 0):
                            sp.wait_ge(s_sc, b * 2 * STEPS - 2 * STEPS + 2 * NT * (g + 1))
                        for h in range(HG * g, HG * g + HG):
                            c, row, at0 = h * DH // P, h * DH % P, 64 * (h % 2)
                            for k, part in enumerate((0, 1, 0)):
                                sp.dma_start(q_st[at0 + DH * k:at0 + DH * (k + 1), h, :],
                                             q_hl[row:row + DH, part, c, :]).then_inc(s_st[g], 16)
                            for k, part in enumerate((0, 0, 1)):
                                sp.dma_start(k_st[at0 + DH * k:at0 + DH * (k + 1), h // 2, :],
                                             k_hl[row:row + DH, part, c, :]).then_inc(s_st[g], 16)
                            if shifted:
                                sp.dma_start(q_st[at0 + 3 * DH:at0 + 3 * DH + 2, h, :], zrow[:, :]).then_inc(s_st[g], 16)

                    sp.wait_ge(s_prepd, V_k)
                    for g in range(G):
                        stacks(0, g)

                    def store(b):
                        rows = out_rows[bass.ds(b * LQ, LQ), :].rearrange("(t p) d -> p t d", p=P)
                        sp.wait_ge(s_epid, b * NEP + nT_k)
                        sp.dma_start(rows, x1[:, :, :]).then_inc(s_x1o, 16)
                        rows = xn2_dram[bass.ds(b * LQ, LQ), :].rearrange("(t p) d -> p t d", p=P)
                        sp.wait_ge(s_nx, b + 1)
                        sp.dma_start(rows, xn2[:, :, :]).then_inc(s_xno, 16)

                    def body(b, first, final):
                        if not final:
                            sp.wait_ge(s_prep, b * NP + K_k)
                            sp.wait_ge(s_v, b * G + G)
                            sp.dma_start(x_sb[:, :, :],
                                         x[bass.ds(b + 1, 1)].rearrange("o (t p) d -> p (o t) d", p=P)).then_inc(s_x, 16)
                            sp.dma_start(c_sb[:, 0:NT - 1, :],
                                         ctx[bass.ds(b + 1, 1), 0:(NT - 1) * P].rearrange("o (t p) d -> p (o t) d", p=P)).then_inc(s_c, 16)
                            sp.dma_start(c_sb[0:LAST, NT - 1, :],
                                         ctx[bass.ds(b + 1, 1), (NT - 1) * P:LK].rearrange("o p d -> p (o d)")).then_inc(s_c, 16)
                        if not first:
                            store(b - 1)
                            sp.wait_ge(s_x1o, 16 * b)
                            sp.wait_ge(s_xno, 16 * b)
                        sp.dma_start(x1[:, :, :], x[bass.ds(b, 1)].rearrange("o (t p) d -> p (o t) d", p=P)).then_inc(s_xr, 16)
                        if not final:
                            sp.wait_ge(s_prepd, (b + 1) * NP + V_k)
                            for g in range(G):
                                stacks(b + 1, g)

                    body(0, True, False)
                    with sp.Fori(1, B - 1) as b:
                        body(b, False, False)
                    body(B - 1, False, True)
                    store(B - 1)
                    sp.wait_ge(s_x1o, 16 * B)
                    sp.wait_ge(s_xno, 16 * B)

                @program(block.gpsimd)
                def _(pool):
                    pool.memset(ident[:, :], 0.0).then_inc(s_const, 1)
                    pool.memset(tri[:, :], 1.0).then_inc(s_const, 1)
                    pool.memset(ones_b[:, :], 1.0).then_inc(s_const, 1)
                    pool.memset(half[:, :], -0.5).then_inc(s_const, 1)
                    pool.memset(v_raw[:, :, :], 0.0).then_inc(s_const, 1)
                    pool.memset(k_hl[:, :, :, LK:LK + 1], 0.0).then_inc(s_const, 1)
                    pool.memset(v_st[:, :, :], 1.0).then_inc(s_const, 1)
                    pool.iota(iota8[:, :, :], [[0, NQ], [1, NE]], base=0, channel_multiplier=0,
                              allow_small_or_imprecise_dtypes=True).then_inc(s_const, 1)
                    pool.wait_ge(s_const, 9)
                    pool.affine_select(out=ident[:, :], in_=ident[:, :], compare_op=ALU.not_equal, fill=1.0,
                                       base=0, pattern=[[-1, P]], channel_multiplier=1).then_inc(s_const, 1)
                    pool.affine_select(out=tri[:, :], in_=tri[:, :], compare_op=ALU.is_gt, fill=0.0,
                                       base=0, pattern=[[1, P]], channel_multiplier=-1).then_inc(s_const, 1)
                    pool.memset(q_st[:, :, :], 0.0).then_inc(s_const, 1)
                    if shifted:
                        pool.memset(zrow[:, :], 0.0).then_inc(s_const, 1)
                    else:
                        pool.memset(onec[:, :], 1.0).then_inc(s_const, 1)
                    pool.wait_ge(s_const, NCONST)

                    def ln1(b):
                        pool.wait_ge(s_mv1, b + 1)
                        pool.tensor_tensor(rstd1[:, :], mv1[:, :, 1], half[:, :], ALU.pow).then_inc(s_r1, 1)

                    def place(b, g):
                        if not (isinstance(b, int) and b == 0):
                            pool.wait_ge(s_pv, b * STEPS - STEPS + NT * (g + 1))
                        stand(pool, s_past_p)
                        w = slice(HG * g * VW, HG * (g + 1) * VW)
                        dst = v_st[:, :, w].rearrange("p t (h c) -> p t h c", h=HG)[:, :, :, 0:DH]
                        src = v_raw[:, :, HG * g * DH:HG * (g + 1) * DH].rearrange("p t (h c) -> p t h c", h=HG)
                        for t in range(NT):
                            ins = pool.tensor_copy(dst[:, t], src[:, t])
                        ins.then_inc(s_v, 1)

                    def ln2(b):
                        pool.wait_ge(s_xr, 16 * b + 16)
                        for t in range(NQ):
                            ins = pool.tensor_tensor(x1[:, t, :], x1[:, t, :], bob[:, :], ALU.add)
                        ins.then_inc(s_bo, 1)
                        pool.wait_ge(s_mv2, b + 1)
                        pool.tensor_tensor(rstd2[:, :], mv2[:, :, 1], half[:, :], ALU.pow).then_inc(s_r2, 1)

                    pool.wait_ge(s_w, NW)
                    ln1(0)
                    pool.wait_ge(s_prepd, NP)
                    for g in range(G):
                        place(0, g)

                    def body(b, first, final):
                        if not first:
                            ln2(b - 1)
                        if not final:
                            ln1(b + 1)
                            pool.wait_ge(s_prepd, (b + 2) * NP)
                            for g in range(G):
                                place(b + 1, g)

                    body(0, True, False)
                    with pool.Fori(1, B - 1) as b:
                        body(b, False, False)
                    body(B - 1, False, True)
                    ln2(B - 1)

                @program(block.scalar)
                def _(act):
                    def body(b, first):
                        for n in range(2 * STEPS):
                            u, j = n // 2, n % 2
                            if shifted and n % (2 * NT) == 0:
                                shift_rows(b, u // NT)
                            rows = P if u % NT < NT - 1 else LAST
                            act.wait_ge(s_sc, b * 2 * STEPS + n + 1)
                            if not (first and u < 2):
                                act.wait_ge(s_pv, b * STEPS + u - 1)
                            act.activation(pr[0:rows, u % 2, j, :], sc[0:rows, n % 3, :], ACT.Exp,
                                           scale=SCALE).then_inc(s_exp, 1)
                            if n == 2 * GATE_EXP and not first:
                                gate(b - 1)

                    def shift_rows(b, g):
                        act.wait_ge(s_md, (b * G + g + 1) * (KM + 1))
                        for k in range(KM):
                            h = HG * g + k // NQ
                            row, cols = 64 * (h % 2) + 3 * DH, slice(k % NQ * P, (k % NQ + 1) * P)
                            for part in range(2):
                                act.dma_start(q_st[row + part:row + part + 1, h, cols],
                                              mrow[k:k + 1, part, :]).then_inc(s_ms, 16)

                    def gate(b):
                        act.wait_ge(s_z, b + 1)
                        act.activation(ez[:, :, :], zz[:, :, :], ACT.Exp).then_inc(s_ez, 1)

                    body(0, True)
                    with act.Fori(1, B) as b:
                        body(b, False)
                    gate(B - 1)

                @program(block.tensor)
                def _(pe):
                    def prep(b, k):
                        kind, *arg = PREP[k]
                        if kind == "xT":
                            c, = arg
                            if c == 0:
                                pe.wait_ge(s_xn, b + 1)
                            for t in range(NQ):
                                ins = pe.transpose(pm[:, t * P:(t + 1) * P], x_sb[:, t, c * P:(c + 1) * P], ident[:, :])
                        elif kind == "Q":
                            c, = arg
                            for k2 in range(ND):
                                ins = pe.matmul(pm[:, 0:LQ], wq[:, k2, c * P:(c + 1) * P], xT[:, k2, :],
                                                start=(k2 == 0), stop=(k2 == ND - 1))
                        elif kind == "cT":
                            n, = arg
                            if n == 0:
                                pe.wait_ge(s_c, b * 32 + 32)
                            for t in range(4 * n, min(4 * n + 4, NT)):
                                w = P if t < NT - 1 else LAST
                                ins = pe.transpose(pm[:, (t - 4 * n) * P:(t - 4 * n) * P + w], c_sb[0:w, t, :],
                                                   ident[0:w, 0:w])
                        elif kind == "K":
                            c, n = arg
                            w = min(MM, LK - n * MM)
                            ins = pe.matmul(pm[:, 0:w], wk[:, c * P:(c + 1) * P], cT[:, n * MM:n * MM + w],
                                            start=True, stop=True)
                        else:
                            n, = arg
                            for t in range(2 * n, min(2 * n + 2, NT)):
                                w = P if t < NT - 1 else LAST
                                ins = pe.matmul(pm[0:w, (t - 2 * n) * D:(t - 2 * n + 1) * D], cT[:, t * P:t * P + w],
                                                wv[:, :], start=True, stop=True)
                        ins.then_inc(s_prep, 1)

                    def epi(b, k):
                        kind, *arg = EPI[k]
                        if kind == "O":
                            n, = arg
                            if n == 0:
                                pe.wait_ge(s_at, b * (G // 2) + G // 2)
                            for t in range(2 * n, 2 * n + 2):
                                for p2 in range(G // 2):
                                    ins = pe.matmul(pm[:, (t % 2) * D:(t % 2 + 1) * D], at[:, p2, t * P:(t + 1) * P],
                                                    wo[:, p2, :], start=(p2 == 0), stop=(p2 == G // 2 - 1))
                        elif kind == "nT":
                            c, = arg
                            if c == 0:
                                pe.wait_ge(s_n, b + 1)
                            for t in range(NQ):
                                ins = pe.transpose(pm[:, t * P:(t + 1) * P], xn2[:, t, c * P:(c + 1) * P], ident[:, :])
                        else:
                            for t in range(NQ):
                                for c in range(ND):
                                    ins = pe.matmul(pm[:, t * NE:(t + 1) * NE], nT[:, c, t * P:(t + 1) * P],
                                                    wg[:, c, :], start=(c == 0), stop=(c == ND - 1))
                        ins.then_inc(s_epi, 1)

                    def pv(b, u, first):
                        g, t = u // NT, u % NT
                        rows = P if t < NT - 1 else LAST
                        pe.wait_ge(s_exp, b * 2 * STEPS + 2 * u + 2)
                        if t == 0:
                            pe.wait_ge(s_v, b * G + min(g + 2, G))
                            if not (first and g == 0):
                                pe.wait_ge(s_oc, b * G + g)
                        for h in range(HG):
                            c = (HG * g + h) * VW
                            ins = pe.matmul(po[32 * h:32 * h + 32, 0:LQ], v_st[0:rows, t, c:c + 32],
                                            pr[0:rows, u % 2, h // 2, (h % 2) * LQ:(h % 2 + 1) * LQ],
                                            start=(t == 0), stop=(t == NT - 1), tile_position=(0, 32 * h))
                        ins.then_inc(s_pv, 1)

                    def maxima(b, g, u, first):
                        if u > 0 or not first:
                            pe.wait_ge(s_exp, b * 2 * STEPS + 2 * u)
                        done = (b * G + g) * (KM + 1)
                        for k in range(KM):
                            h = HG * g + k // NQ
                            if k > 0:
                                pe.wait_ge(s_md, done + k)
                            for n in range(NKC):
                                w = min(MM, LK + LK % 2 - n * MM)
                                ins = pe.matmul(sflat[:, n * MM:n * MM + w],
                                                r(q_st[:, h, k % NQ * P:(k % NQ + 1) * P]),
                                                r(k_st[:, h // 2, n * MM:n * MM + w]), start=True, stop=True)
                            ins.then_inc(s_mr, 1)
                        pe.wait_ge(s_md, done + KM)
                        pe.transpose(sflat[0:KM, 5 * MM:5 * MM + P], mxv[:, :], ident[:, :]).then_inc(s_mr, 1)
                        pe.wait_ge(s_ms, (b * G + g + 1) * KM * 2 * 16)
                        pe.wait_ge(s_md, done + KM + 1)

                    def body(b, first, final):
                        for u in range(STEPS):
                            g, t = u // NT, u % NT
                            if t == 0:
                                pe.wait_ge(s_st[g], b * STK + STK)
                                if shifted:
                                    maxima(b, g, u, first)
                            rows = P if t < NT - 1 else LAST
                            for j in range(2):
                                n = 2 * u + j
                                if n >= 3:
                                    pe.wait_ge(s_exp, b * 2 * STEPS + n - 2)
                                elif not first:
                                    before = max(m for m in range(2 * STEPS) if m % 3 == n)
                                    pe.wait_ge(s_exp, b * 2 * STEPS - 2 * STEPS + before + 1)
                                for h in (HG * g + 2 * j, HG * g + 2 * j + 1):
                                    ins = pe.matmul(sc[0:rows, n % 3, (h % 2) * MM:(h % 2) * MM + LQ],
                                                    r(k_st[:, h // 2, t * P:t * P + rows]), r(q_st[:, h, :]),
                                                    start=True, stop=True)
                                ins.then_inc(s_sc, 1)
                            if u > 0:
                                pv(b, u - 1, first)
                            elif not first:
                                pv(b - 1, STEPS - 1, False)
                            if u in late and not first:
                                if late[u] == 0:
                                    pe.wait_ge(s_prepd, b * NP + NP)
                                else:
                                    pe.wait_ge(s_epid, (b - 1) * NEP + late[u])
                                epi(b - 1, late[u])
                            if u in prep_at and not final:
                                k = prep_at[u]
                                if k == 0 and not first:
                                    pe.wait_ge(s_epid, b * NEP)
                                pe.wait_ge(s_prepd, (b + 1) * NP + k)
                                prep(b + 1, k)

                    pe.wait_ge(s_const, NCONST)
                    pe.wait_ge(s_w, NW)
                    for k in range(NP):
                        if k:
                            pe.wait_ge(s_prepd, k)
                        prep(0, k)
                    body(0, True, False)
                    with pe.Fori(1, B - 1) as b:
                        body(b, False, False)
                    body(B - 1, False, True)
                    pv(B - 1, STEPS - 1, False)
                    for k in range(NEP):
                        pe.wait_ge(s_epid, (B - 1) * NEP + k)
                        epi(B - 1, k)
                    if not shifted:
                        pe.wait_ge(s_epid, (B - 1) * NEP + NEP)
                        pe.wait_ge(s_ok, 1)
                        pe.matmul(pm[0:1, 0:1], okc[:, 0:1], onec[:, :], start=True, stop=True).then_inc(s_okp, 1)

                @program(block.vector)
                def _(dve):
                    chained = [0]

                    counted = [0]
                    links = LINKS + (G if shifted else 3 * G + 2)

                    def link(ins):
                        ins.then_inc(s_dve, 1)
                        chained[0] = chained[0] + 1
                        counted[0] += 1
                        dve.wait_ge(s_dve, chained[0])

                    def stats(src, t, st):
                        return dve.bn_stats(st[:, t, :], src[:, t, :])

                    def moments(st, mv, signal):
                        stand(dve, s_past)
                        for t in range(NQ):
                            ins = dve.bn_aggr(mv[:, t, :], st[:, t, :])
                        link(ins)
                        dve.tensor_scalar(mv[:, :, 1], mv[:, :, 1], EPS, None, ALU.add).then_inc(signal, 1)

                    def ln1_stats(b):
                        dve.wait_ge(s_x, b * 16 + 16)
                        for t in range(NQ):
                            ins = stats(x_sb, t, st1)
                        link(ins)
                        moments(st1, mv1, s_mv1)

                    def ln1_apply(b):
                        dve.wait_ge(s_mv1, b + 1)
                        dve.wait_ge(s_r1, b + 1)
                        for t in range(NQ):
                            ins = dve.tensor_scalar(x_sb[:, t, :], x_sb[:, t, :], mv1[:, t, 0:1], rstd1[:, t:t + 1],
                                                    ALU.subtract, ALU.mult)
                        ins.then_inc(s_xn, 1)

                    def split(bank, bias, hi, lo):
                        link(dve.tensor_scalar(r(hi), bank, bias, None, ALU.add))
                        dve.scalar_tensor_tensor(r(lo), bank, bias, hi, ALU.add, ALU.subtract).then_inc(s_prepd, 1)

                    def prep(b, k):
                        kind, *arg = PREP[k]
                        dve.wait_ge(s_prep, b * NP + k + 1)
                        if kind == "xT":
                            dve.tensor_copy(xT[:, arg[0], :], pm[:, 0:LQ]).then_inc(s_prepd, 1)
                        elif kind == "Q":
                            c, = arg
                            if c == 0 and not (isinstance(b, int) and b == 0):
                                for g in range(G):
                                    dve.wait_ge(s_st[g], b * STK)
                            split(pm[:, 0:LQ], bqc[:, c:c + 1], q_hl[:, 0, c, :], q_hl[:, 1, c, :])
                        elif kind == "cT":
                            n, = arg
                            w = min(MM, LK - n * MM)
                            dve.tensor_copy(cT[:, n * MM:n * MM + w], pm[:, 0:w]).then_inc(s_prepd, 1)
                        elif kind == "K":
                            c, n = arg
                            w = min(MM, LK - n * MM)
                            at0 = slice(n * MM, n * MM + w)
                            split(pm[:, 0:w], bkc[:, c:c + 1], k_hl[:, 0, c, at0], k_hl[:, 1, c, at0])
                        else:
                            n, = arg
                            if n == 0 and not (isinstance(b, int) and b == 0):
                                dve.wait_ge(s_v, b * G)
                            t0, t1 = 2 * n, min(2 * n + 2, NT)
                            w = P if t1 < NT or t1 - t0 == 2 else LAST
                            assert t1 < NT or t1 - t0 == 1
                            for t in range(t0, t1):
                                ins = dve.tensor_tensor(v_raw[0:w, t, :], pm[0:w, (t - t0) * D:(t - t0 + 1) * D],
                                                        bvb[0:w, :], ALU.add)
                            ins.then_inc(s_prepd, 1)

                    def normalise(b, g):
                        dve.wait_ge(s_pv, b * STEPS + NT * (g + 1))
                        dve.transpose(o_t[:, :, :].rearrange("p a c -> p (a c)"), po[:, 0:LQ]).then_inc(s_oc, 1)
                        dve.wait_ge(s_oc, b * G + g + 1)
                        link(dve.reciprocal(rec[:, :], o_t[:, :, DH]))
                        i = g % 2
                        link(dve.tensor_tensor(o_n[:, :, DH * i:DH * (i + 1)], o_t[:, :, 0:DH],
                                               rec[:, :].rearrange("p (a o) -> p a o", o=1).broadcast_to([P, NB32, DH]),
                                               ALU.mult))
                        if i == 1:
                            dve.transpose(at[:, g // 2, :], o_n[:, :, :].rearrange("p a c -> p (a c)")).then_inc(s_at, 1)
                            dve.wait_ge(s_at, b * (G // 2) + g // 2 + 1)
                        if not shifted:
                            link(dve.tensor_scalar(rok[:, :], rec[:, :], SUM_REACH, None, ALU.is_lt))
                            link(dve.scalar_tensor_tensor(rok[:, :], rec[:, :], 1.0 / SUM_REACH, rok[:, :],
                                                          ALU.is_gt, ALU.mult))
                            link(dve.tensor_reduce(red[:, 0, bass.ds(b * G + g, 1)], rok[:, :], AX.X, ALU.min,
                                                   negate=True))

                    def finite(b):
                        link(dve.tensor_scalar(rok[:, 0:NQ], mv2[:, :, 1], OUT_REACH, None, ALU.is_lt))
                        link(dve.tensor_reduce(red[:, 1, bass.ds(b * G, 1)], rok[:, 0:NQ], AX.X, ALU.min, negate=True))

                    def verdict():
                        link(dve.tensor_reduce(okc[:, 0:1], red[:, :, :], AX.XY, ALU.max))
                        dve.tensor_scalar(okc[:, 0:1], okc[:, 0:1], -0.5, None, ALU.is_gt).then_inc(s_ok, 1)
                        dve.wait_ge(s_okp, 1)
                        dve.tensor_copy(redo[0:1, 0:1], pm[0:1, 0:1]).then_inc(s_redo, 1)

                    def maxima(b, g):
                        done = (b * G + g) * (KM + 1)
                        for k in range(KM):
                            dve.wait_ge(s_mr, done + k + 1)
                            dve.tensor_reduce(mxv[:, k:k + 1], sflat[:, 0:LK], AX.X, ALU.max).then_inc(s_md, 1)
                        dve.wait_ge(s_mr, done + KM + 1)
                        bank = sflat[0:KM, 5 * MM:5 * MM + P]
                        link(dve.tensor_scalar(r(mrow[:, 0, :]), bank, -1.0, None, ALU.mult))
                        dve.scalar_tensor_tensor(r(mrow[:, 1, :]), bank, -1.0, mrow[:, 0, :], ALU.mult,
                                                 ALU.subtract).then_inc(s_md, 1)

                    def epi(b, k):
                        kind, *arg = EPI[k]
                        dve.wait_ge(s_epi, b * NEP + k + 1)
                        if kind == "O":
                            n, = arg
                            if n == 0:
                                dve.wait_ge(s_bo, b + 1)
                            t2 = slice(2 * n, 2 * n + 2)
                            dve.tensor_tensor(x1[:, t2, :], pm[:, :].rearrange("p (t d) -> p t d", t=2), x1[:, t2, :],
                                              ALU.add).then_inc(s_epid, 1)
                            dve.wait_ge(s_epid, b * NEP + k + 1)
                            for t in range(2 * n, 2 * n + 2):
                                ins = stats(x1, t, st2)
                            link(ins)
                            if n == NQ // 2 - 1:
                                moments(st2, mv2, s_mv2)
                        elif kind == "nT":
                            dve.tensor_copy(nT[:, arg[0], :], pm[:, 0:LQ]).then_inc(s_epid, 1)
                        else:
                            gate(b, k)

                    def ln2_apply(b):
                        dve.wait_ge(s_mv2, b + 1)
                        if not shifted:
                            finite(b)
                        dve.wait_ge(s_r2, b + 1)
                        for t in range(NQ):
                            ins = dve.tensor_scalar(xn2[:, t, 0:D], x1[:, t, :], mv2[:, t, 0:1], rstd2[:, t:t + 1],
                                                    ALU.subtract, ALU.mult)
                        ins.then_inc(s_n, 1)

                    def gate(b, k):
                        dve.tensor_copy(lg[:, :, :], pm[:, 0:NQ * NE].rearrange("p (t e) -> p t e", t=NQ)).then_inc(s_epid, 1)
                        dve.wait_ge(s_epid, b * NEP + k + 1)
                        stand(dve, s_past)
                        for t in range(NQ):
                            ins = dve.max(mx[:, t, :], lg[:, t, :])
                        link(ins)
                        dve.tensor_tensor(zz[:, :, :], lg[:, :, :], mx[:, :, 0:1].broadcast_to([P, NQ, NE]),
                                          ALU.subtract).then_inc(s_z, 1)
                        for t in range(NQ):
                            ins = dve.max_index(mi[:, t, :], mx[:, t, :], lg[:, t, :])
                        link(ins)
                        link(dve.tensor_copy(mif[:, :, :], mi[:, :, 0:2]))
                        for k2 in range(2):
                            ins = dve.tensor_tensor(oh[:, k2, :, :], iota8[:, :, :],
                                                    mif[:, :, k2:k2 + 1].broadcast_to([P, NQ, NE]), ALU.is_equal)
                        link(ins)

                    def gates(b):
                        dve.wait_ge(s_ez, b + 1)
                        link(dve.tensor_reduce(gs[:, :], ez[:, :, :], AX.X, ALU.add))
                        link(dve.reciprocal(gs[:, :], gs[:, :]))
                        link(dve.tensor_tensor(ez[:, :, :], ez[:, :, :],
                                               gs[:, :].rearrange("p (t o) -> p t o", o=1).broadcast_to([P, NQ, NE]), ALU.mult))
                        link(dve.tensor_tensor(lg[:, :, :], oh[:, 0, :, :], oh[:, 1, :, :], ALU.add))
                        dve.tensor_tensor(xn2[:, :, D:XW], ez[:, :, :], lg[:, :, :], ALU.mult).then_inc(s_nx, 1)
                        link(dve.tensor_copy(onehot[:, :, bass.ds(b * NQ, NQ), :], oh[:, :, :, :]))

                    def body(b, first, final):
                        for u in range(STEPS):
                            if shifted and u % NT == 0:
                                maxima(b, u // NT)
                            if u % NT == 1:
                                if u > 1:
                                    normalise(b, u // NT - 1)
                                elif not first:
                                    normalise(b - 1, G - 1)
                            if u in late and not first:
                                epi(b - 1, late[u])
                            if u in prep_at and not final:
                                prep(b + 1, prep_at[u])
                            if u == 8 and not first:
                                ln2_apply(b - 1)
                            if u == LN1_STATS and not final:
                                ln1_stats(b + 1)
                            if u == GATE_END and not first:
                                gates(b - 1)
                            if u == LN1_APPLY and not final:
                                ln1_apply(b + 1)

                    dve.memset(k_st[:, :, :], 1.0).then_inc(s_const, 1)
                    if not shifted:
                        link(dve.memset(red[:, :, :], -1.0))
                    dve.wait_ge(s_w, NW)
                    dve.wait_ge(s_const, NCONST)
                    ln1_stats(0)
                    ln1_apply(0)
                    for k in range(NP):
                        prep(0, k)
                    body(0, True, False)
                    start = chained[0]
                    with dve.Fori(1, B - 1) as b:
                        chained[0] = (b - 1) * links + start
                        counted[0] = 0
                        body(b, False, False)
                        assert counted[0] == links, counted[0]
                    chained[0] = (B - 2) * links + start
                    body(B - 1, False, True)
                    normalise(B - 1, G - 1)
                    for k in range(NEP):
                        epi(B - 1, k)
                        if k == O_k + 1:
                            ln2_apply(B - 1)
                    gates(B - 1)
                    if not shifted:
                        verdict()

        attention(False)
        attention(True)

        NSL = CAPACITY // P
        NPAIR = 2 * NTT
        CH = min(16, NTT & -NTT)
        NCH = NPAIR // CH
        COLS = NE * NSL
        with ExitStack() as es2:
            def sb2(name, shape, dt=F32):
                return es2.enter_context(nc.sbuf_tensor(name, shape, dt))

            def sem2(name):
                return es2.enter_context(nc.semaphore(name))

            iota_a = sb2("iota_a", [P, P])
            iota_t = sb2("iota_t", [P, NTT])
            iota_p = sb2("iota_p", [P, 1])
            iota_e = sb2("iota_e", [P, NTT, NE])
            tot = sb2("tot", [P, NTT, NE])
            inc = sb2("inc", [P, NTT, NE])
            pos = sb2("pos", [P, NTT, NE])
            one = sb2("one", [P, NTT])
            tmp = sb2("tmp", [P, 2, NTT, NE])
            pk = sb2("pk", [P, 2, NTT])
            ek = sb2("ek", [P, 2, NTT])
            pi = sb2("pi", [P, 2, NTT], I32)
            li = sb2("li", [P, 2, NTT], I32)
            af = sb2("af", [P, 2, NTT])
            bf = sb2("bf", [P, 2, NTT])
            A = sb2("A", [P, NPAIR, P], BF16)
            Bq = sb2("Bq", [P, CH, COLS], BF16)
            Bt = sb2("Bt", [P, NPAIR, 2, COLS], BF16)
            tab = sb2("tab", [P, 2, COLS])
            occ = sb2("occ", [P, COLS])
            gidx = sb2("gidx", [P, COLS + NSL], I32)
            sidx = sb2("sidx", [P, COLS], I32)
            gst = sb2("gst", [P, 2, NSL], I32)
            sst = sb2("sst", [P, 2, NSL], I32)
            w1 = sb2("w1", [P, 2, ND, 2 * FF])
            w2 = sb2("w2", [P, 2, NF, D])
            xg = [[sb2(f"xg{i}_{c}", [P, XW]) for c in range(NSL)] for i in range(2)]
            gw = sb2("gw", [P, 2, NSL])
            xt = sb2("xt", [P, 2, ND, CAPACITY])
            sa = sb2("sa", [P, 2, MM])
            ht = sb2("ht", [P, NF, CAPACITY])
            ys = [[sb2(f"y{i}_{c}", [P, D]) for c in range(NSL)] for i in range(2)]

            hp = es2.enter_context(nc.psum_tensor("h_banks", [P, 2, 2, MM], F32))
            tp = es2.enter_context(nc.psum_tensor("t_banks", [P, 2, MM], F32))
            yp = es2.enter_context(nc.psum_tensor("y_banks", [P, 2, MM], F32))

            s_i = sem2("iotas_made")
            s_cum = sem2("counts_ready")
            s_ab = sem2("onehots_ready")
            s_tab = sem2("table_ready")
            s_idx = sem2("indices_ready")
            s_wt = [sem2(f"expert_weights{i}") for i in range(2)]
            s_stg = sem2("gather_indices_staged")
            s_ssg = sem2("scatter_indices_staged")
            s_g = [sem2(f"rows_gathered{i}") for i in range(2)]
            s_t = sem2("rows_transposed")
            s_td = sem2("rows_T_copied")
            s_a = sem2("hidden_ready")
            s_si = sem2("silu_ready")
            s_h = sem2("gated_ready")
            s_y = sem2("y_ready")
            s_ye = sem2("y_scaled")
            s_gw = sem2("gates_ready")
            s_yf = sem2("experts_added")
            s_add = sem2("y_added")
            s_d2 = sem2("dve_step2")
            s_past2 = sem2("pool_waits_passed2")
            block = es2.enter_context(nc.Block())

            H2 = CAPACITY // MM
            UN = H2 * NF
            NTI = H2 * ND

            ORDER = ([("h", k) for k in range(NF + 1)] + [("y", k) for k in range(MM // P)]
                     + [("h", k) for k in range(NF + 1, UN)] + [("t", k) for k in range(NTI)]
                     + [("y", k) for k in range(MM // P, NSL)])

            @block.sync
            def _(sp):
                def load(e, i):
                    sp.dma_start(w1[:, i, :, :],
                                 c_fc[bass.ds(e, 1)].rearrange("o (c p) f -> p (o c) f", p=P)).then_inc(s_wt[i], 16)
                    sp.dma_start(w2[:, i, :, :],
                                 c_proj[bass.ds(e, 1)].rearrange("o (c p) f -> p (o c) f", p=P)).then_inc(s_wt[i], 16)

                load(0, 0)
                load(1, 1)
                with sp.Fori(0, NE // 2 - 1) as pair:
                    e = pair * 2
                    for i in range(2):
                        sp.wait_ge(s_y, (e + i) * NSL + NSL)
                        load(e + i + 2, i)

            @block.gpsimd
            def _(pool):
                pool.iota(iota_a[:, :], [[1, P]], base=0, channel_multiplier=0,
                          allow_small_or_imprecise_dtypes=True).then_inc(s_i, 1)
                pool.iota(iota_t[:, :], [[1, NTT]], base=1, channel_multiplier=0,
                          allow_small_or_imprecise_dtypes=True).then_inc(s_i, 1)
                pool.iota(iota_p[:, :], [[0, 1]], base=0, channel_multiplier=1,
                          allow_small_or_imprecise_dtypes=True).then_inc(s_i, 1)
                pool.iota(iota_e[:, :, :], [[0, NTT], [1, NE]], base=0, channel_multiplier=0,
                          allow_small_or_imprecise_dtypes=True).then_inc(s_i, 1)
                pool.memset(one[:, :], 1.0).then_inc(s_i, 1)
                pool.memset(gidx[:, COLS:], 0).then_inc(s_i, 1)
                def gather(e, i):
                    stand(pool, s_past2)
                    pool.tensor_copy(gst[:, i, :], gidx[:, bass.ds(e * NSL, NSL)]).then_inc(s_stg, 1)
                    pool.wait_ge(s_stg, e + 1)
                    stand(pool, s_past2)
                    for c in range(NSL):
                        pool.indirect_dma_start(out=xg[i][c][:, :], out_offset=None, in_=xn2_dram[:, :],
                                                in_offset=bass.IndirectOffsetOnAxis(ap=gst[:, i, c:c + 1], axis=0),
                                                bounds_check=NTOK - 1, oob_is_err=False).then_inc(s_g[i], 16)

                for c in range(2):
                    pool.sem_inc(s_yf, 1)
                pool.wait_ge(s_idx, 1)
                gather(0, 0)
                with pool.Fori(0, NE // 2) as pair:
                    e2 = pair * 2
                    for i in range(2):
                        e = e2 + i
                        pool.wait_ge(s_t, e * NTI + NTI)
                        pool.wait_ge(s_gw, e + 1)
                        gather(e + 1, 1 - i)
                        pool.tensor_copy(sst[:, i, :], sidx[:, bass.ds(e * NSL, NSL)]).then_inc(s_ssg, 1)
                        pool.wait_ge(s_ssg, e + 1)
                        stand(pool, s_past2)
                        for c in range(NSL):
                            pool.wait_ge(s_ye, e * NSL + c + 3)
                            stand(pool, s_past2)
                            pool.indirect_dma_start(out=out_rows, in_=ys[i][c][:, :],
                                                    out_offset=bass.IndirectOffsetOnAxis(ap=sst[:, i, c:c + 1], axis=0),
                                                    in_offset=None, bounds_check=NTOK - 1, oob_is_err=False,
                                                    compute_op=ALU.add).then_inc(s_add, 16)
                        pool.wait_ge(s_add, e * NSL * 16 + NSL * 16)
                        pool.sem_inc(s_yf, 1)

            @block.scalar
            def _(act):
                for c in range(2):
                    act.sem_inc(s_ye, 1)

                def silu(e, m):
                    act.wait_ge(s_a, e * UN + m + 1)
                    act.wait_ge(s_h, e * UN + m + 1)
                    act.activation(sa[:, m % 2, :], hp[:, m % 2, 0, :], ACT.Silu).then_inc(s_si, 1)

                def scale(e, i, c):
                    act.wait_ge(s_y, e * NSL + c + 1)
                    if c == 0:
                        act.wait_ge(s_gw, e + 1)
                        act.wait_ge(s_yf, e + 1)
                    act.activation(ys[i][c][:, :], yp[:, c % 2, 0:D], ACT.Copy,
                                   scale=gw[:, i, c:c + 1]).then_inc(s_ye, 1)

                with act.Fori(0, NE // 2) as pair:
                    e2 = pair * 2
                    for i in range(2):
                        e = e2 + i
                        for kind, k in ORDER:
                            if kind == "h":
                                silu(e, k)
                            elif kind == "y":
                                scale(e, i, k)

            @block.tensor
            def _(pe):
                def table():
                    pe_oh = onehot[:, :, :, :].rearrange("p k t e -> p k (t e)")
                    for k in range(2):
                        pe.matmul(hp[:, 0, 0, 0:NTT * NE], tri[:, :], pe_oh[:, k, :], start=(k == 0), stop=(k == 1))
                    for k in range(2):
                        ins = pe.matmul(hp[:, 0, 1, 0:NTT * NE], ones_b[:, :], pe_oh[:, k, :],
                                        start=(k == 0), stop=(k == 1))
                    ins.then_inc(s_cum, 1)
                    for n in range(NPAIR):
                        if n % CH == 0:
                            pe.wait_ge(s_ab, n // CH + 1)
                        ins = pe.matmul(tp[:, 0, 0:2 * COLS], A[:, n, :],
                                        Bt[:, n, :, :].rearrange("p a c -> p (a c)"),
                                        start=(n == 0), stop=(n == NPAIR - 1))
                    ins.then_inc(s_tab, 1)

                def turn(e, i, k):
                    h, c = k // ND, k % ND
                    pe.wait_ge(s_td, e * NTI + k)
                    for j in range(MM // P):
                        ins = pe.transpose(tp[:, k % 2, j * P:(j + 1) * P],
                                           xg[i][h * (MM // P) + j][:, c * P:(c + 1) * P], ident[:, :])
                    ins.then_inc(s_t, 1)

                def hidden(e, i, m):
                    h, f = m // NF, m % NF
                    pe.wait_ge(s_h, e * UN + m + 1)
                    for part in range(2):
                        for c in range(ND):
                            o = part * FF + f * P
                            ins = pe.matmul(hp[:, m % 2, part, :], w1[:, i, c, o:o + P],
                                            xt[:, i, c, h * MM:(h + 1) * MM], start=(c == 0), stop=(c == ND - 1))
                    ins.then_inc(s_a, 1)

                def project(e, i, c):
                    if c % (MM // P) == 0:
                        pe.wait_ge(s_h, e * UN + NF * (c // (MM // P) + 1) + 2)
                    pe.wait_ge(s_ye, e * NSL + c + 1)
                    for f in range(NF):
                        ins = pe.matmul(yp[:, c % 2, 0:D], ht[:, f, c * P:(c + 1) * P], w2[:, i, f, :],
                                        start=(f == 0), stop=(f == NF - 1))
                    ins.then_inc(s_y, 1)

                table()
                pe.wait_ge(s_g[0], NSL * 16)
                pe.wait_ge(s_idx, 1)
                for k in range(NTI):
                    turn(0, 0, k)
                with pe.Fori(0, NE // 2) as pair:
                    e2 = pair * 2
                    for i in range(2):
                        e = e2 + i
                        pe.wait_ge(s_wt[i], e2 * 16 + 32)
                        pe.wait_ge(s_td, e * NTI + NTI + 1)
                        for kind, k in ORDER:
                            if kind == "h":
                                hidden(e, i, k)
                            elif kind == "y":
                                project(e, i, k)
                            else:
                                if k == 0:
                                    pe.wait_ge(s_g[1 - i], e2 * (NSL * 8) + NSL * 16 * (1 + i))
                                turn(e + 1, 1 - i, k)

            @block.vector
            def _(dve):
                steps = [0]

                def link(ins):
                    ins.then_inc(s_d2, 1)
                    steps[0] += 1
                    dve.wait_ge(s_d2, steps[0])

                for c in range(2):
                    dve.sem_inc(s_h, 1)
                dve.sem_inc(s_td, 1)
                dve.wait_ge(s_i, 6)
                dve.wait_ge(s_cum, 1)
                flat = [P, NTT, NE]
                link(dve.tensor_copy(tot[:, :, :], hp[:, 0, 1, 0:NTT * NE].rearrange("p (t e) -> p t e", e=NE)))
                for e in range(NE):
                    ins = dve.tensor_tensor_scan(inc[:, :, e], one[:, :], tot[:, :, e], 0.0, ALU.mult, ALU.add)
                link(ins)
                link(dve.tensor_tensor(inc[:, :, :], inc[:, :, :], tot[:, :, :], ALU.subtract))
                link(dve.tensor_tensor(pos[:, :, :], hp[:, 0, 0, 0:NTT * NE].rearrange("p (t e) -> p t e", e=NE),
                                       inc[:, :, :], ALU.add))
                for k in range(2):
                    ins = dve.tensor_tensor(tmp[:, k, :, :], pos[:, :, :], onehot[:, k, :, :], ALU.mult)
                link(ins)
                link(dve.tensor_reduce(pk[:, :, :], tmp[:, :, :, :], AX.X, ALU.add))
                for k in range(2):
                    ins = dve.tensor_tensor(tmp[:, k, :, :], iota_e[:, :, :], onehot[:, k, :, :], ALU.mult)
                link(ins)
                link(dve.tensor_reduce(ek[:, :, :], tmp[:, :, :, :], AX.X, ALU.add))
                link(dve.tensor_copy(pi[:, :, :], pk[:, :, :]))
                link(dve.tensor_scalar(li[:, :, :], pi[:, :, :], P - 1, None, ALU.bitwise_and))
                link(dve.tensor_copy(af[:, :, :], li[:, :, :]))
                link(dve.tensor_scalar(li[:, :, :], pi[:, :, :], 7, None, ALU.logical_shift_right))
                link(dve.tensor_copy(bf[:, :, :], li[:, :, :]))
                link(dve.scalar_tensor_tensor(bf[:, :, :], ek[:, :, :], float(NSL), bf[:, :, :], ALU.mult, ALU.add))
                link(dve.tensor_scalar(pk[:, :, :], pk[:, :, :], float(CAPACITY), 10000.0, ALU.is_ge, ALU.mult))
                link(dve.tensor_tensor(bf[:, :, :], bf[:, :, :], pk[:, :, :], ALU.add))
                for q in range(NCH):
                    k, t0 = q * CH // NTT, q * CH % NTT
                    w = slice(q * CH, (q + 1) * CH)
                    a_ = af[:, k, t0:t0 + CH].rearrange("p (t o) -> p t o", o=1).broadcast_to([P, CH, P])
                    b_ = bf[:, k, t0:t0 + CH].rearrange("p (t o) -> p t o", o=1).broadcast_to([P, CH, COLS])
                    t_ = iota_t[:, t0:t0 + CH].rearrange("p (t o) -> p t o", o=1).broadcast_to([P, CH, COLS])
                    ia = iota_a[:, :].rearrange("p (o c) -> p o c", o=1)
                    dve.tensor_tensor(A[:, w, :], ia.broadcast_to([P, CH, P]), a_, ALU.is_equal)
                    link(dve.tensor_tensor(Bq[:, :, :], ia[:, :, 0:COLS].broadcast_to([P, CH, COLS]), b_, ALU.is_equal))
                    dve.tensor_tensor(Bt[:, w, 0, :], Bq[:, :, :], t_, ALU.mult)
                    dve.tensor_scalar(Bt[:, w, 1, :], Bq[:, :, :], iota_p[:, 0:1], None, ALU.mult).then_inc(s_ab, 1)
                    dve.wait_ge(s_ab, q + 1)
                dve.wait_ge(s_tab, 1)
                link(dve.tensor_copy(tab[:, :, :], tp[:, 0, 0:2 * COLS].rearrange("p (a c) -> p a c", a=2)))
                dve.tensor_scalar(occ[:, :], tab[:, 0, :], 0.5, float(1 << 20), ALU.is_lt, ALU.mult)
                link(dve.scalar_tensor_tensor(tab[:, 1, :], tab[:, 0, :], float(P), tab[:, 1, :], ALU.mult, ALU.add))
                link(dve.tensor_scalar(tab[:, 1, :], tab[:, 1, :], -float(P), 0.0, ALU.add, ALU.max))
                dve.tensor_copy(gidx[:, 0:COLS], tab[:, 1, :])
                link(dve.tensor_tensor(occ[:, :], occ[:, :], tab[:, 1, :], ALU.add))
                dve.tensor_copy(sidx[:, :], occ[:, :]).then_inc(s_idx, 1)

                def turn(e, i, k):
                    h, c = k // ND, k % ND
                    dve.wait_ge(s_t, e * NTI + k + 1)
                    dve.tensor_copy(xt[:, i, c, h * MM:(h + 1) * MM], tp[:, k % 2, :]).then_inc(s_td, 1)

                def gated(e, i, m):
                    h, f = m // NF, m % NF
                    dve.wait_ge(s_si, e * UN + m + 1)
                    dve.tensor_tensor(ht[:, f, h * MM:(h + 1) * MM], sa[:, m % 2, :], hp[:, m % 2, 1, :],
                                      ALU.mult).then_inc(s_h, 1)

                for k in range(NTI):
                    turn(0, 0, k)
                with dve.Fori(0, NE // 2) as pair:
                    e2 = pair * 2
                    for i in range(2):
                        e = e2 + i
                        dve.wait_ge(s_g[i], e2 * (NSL * 8) + NSL * 16)
                        dve.wait_ge(s_ye, e * NSL + 2)
                        for c in range(NSL):
                            ins = dve.tensor_copy(gw[:, i, c:c + 1], xg[i][c][:, bass.ds(D + e, 1)])
                        ins.then_inc(s_gw, 1)
                        for kind, k in ORDER:
                            if kind == "h":
                                gated(e, i, k)
                            elif kind == "t":
                                turn(e + 1, 1 - i, k)


_INS = ["x", "ctx_512", "L0_xattn_Wq", "L0_xattn_bq", "L0_xattn_Wk", "L0_xattn_bk", "L0_xattn_Wv", "L0_xattn_bv",
        "L0_xattn_Wo", "L0_xattn_bo", "L0_ffn_w_gate", "L0_ffn_c_fc", "L0_ffn_c_proj"]


def kernel(**inputs):
    import numpy as _np
    import concourse.bacc as _bacc
    from concourse import mybir as _mybir
    from concourse.bass_utils import run_bass_kernel_spmd as _run

    nc = _bacc.Bacc("TRN2", target_bir_lowering=False, num_devices=1)
    arrays, args = {}, []
    for name in _INS:
        a = _np.ascontiguousarray(inputs[name])
        arrays[f"in_{name}_dram"] = a
        args.append(nc.dram_tensor(f"in_{name}_dram", a.shape, _mybir.dt.from_np(a.dtype), kind="ExternalInput").ap())
    out = nc.dram_tensor("out_0_dram", inputs["x"].shape, _mybir.dt.float32, kind="ExternalOutput").ap()
    build(nc, *args, out)
    r = _run(nc, [arrays], core_ids=[0])
    return r.results[0]["out_0_dram"]
```

```python
import concourse.bass as bass
from concourse import mybir
from contextlib import ExitStack

P = 128
ALU = mybir.AluOpType
ACT = mybir.ActivationFunctionType
AX = mybir.AxisListType
F32 = mybir.dt.float32
F32R = mybir.dt.float32r
BF16 = mybir.dt.bfloat16
I32 = mybir.dt.int32
U32 = mybir.dt.uint32

EPS = 1e-5
DH = 16
HG = 4
CAPACITY = 1024
SUM_REACH = 1e15
OUT_REACH = 1e30
MM = 512


def r(ap):
    return ap.bitcast(F32R)


HALVES = ((0, 0), (0, 1), (1, 0))


def stand(eng, passed):
    eng.sem_inc(passed, 1)


def build(nc, x, ctx, Wq, bq, Wk, bk, Wv, bv, Wo, bo, w_gate, c_fc, c_proj, out):
    B, LQ, D = x.shape
    _, LK, DC = ctx.shape
    H = D // DH
    G = H // HG
    NQ = LQ // P
    ND = D // P
    NT = (LK + P - 1) // P
    LAST = LK - (NT - 1) * P
    NE = w_gate.shape[1]
    NTOK = B * LQ
    NTT = NTOK // P
    FF = c_fc.shape[2] // 2
    NF = FF // P
    XW = D + NE
    SCALE = float(DH) ** -0.5
    STEPS = G * NT
    NB32 = LQ // 32
    NKC = (LK + MM - 1) // MM

    xn2_dram = nc.dram_tensor("xn2_rows", (NTOK, XW), F32, kind="Internal").ap()
    out_rows = out.rearrange("b q d -> (b q) d")

    PREP = ([("xT", c) for c in range(ND)] + [("Q", 0)] + [("cT", k) for k in range(NKC)]
            + [("K", 0, n) for n in range(NKC)] + [("V", k) for k in range(NT)]
            + [item for c in range(1, ND) for item in [("Q", c)] + [("K", c, n) for n in range(NKC)]])
    EPI = [("O", k) for k in range(NQ)] + [("nT", c) for c in range(ND)] + [("lg", t) for t in range(NQ)]
    NP, NEP = len(PREP), len(EPI)
    K_k, V_k = PREP.index(("K", 0, 0)), PREP.index(("V", 0))
    GC = G // ND
    O_k, nT_k, lg_k = EPI.index(("O", 0)), EPI.index(("nT", 0)), EPI.index(("lg", 0))

    late = ({4 + k: O_k + k for k in range(NQ)} | {10 + c: nT_k + c for c in range(ND)}
            | {10 + ND + t: lg_k + t for t in range(NQ)})
    prep_at, q_half = {}, {}
    u = 10 + ND + NQ
    for k in range(NP):
        if PREP[k][0] == "Q":
            for h in range(ND - 1):
                q_half[u] = (k, h)
                u += 1
        prep_at[u] = k
        u += 1
    assert u <= STEPS
    start_at = {1 + k - V_k - NT: k for k in range(V_k + NT, NP)}
    LN1_STATS, LN1_APPLY, GATE_EXP, GATE_END = 12, 14, 18, 18
    BANK = [(n + 2) % 3 if n < 14 else n % 3 for n in range(2 * STEPS)]
    assert (BANK[-1] + 1) % 3 == BANK[0]
    LINKS = 44

    with ExitStack() as es:
        def sb(name, shape, dt=F32):
            return es.enter_context(nc.sbuf_tensor(name, shape, dt))

        def sem(name):
            return es.enter_context(nc.semaphore(name))

        ident = sb("ident", [P, P])
        tri = sb("tri", [P, P], BF16)
        ones_b = sb("ones_b", [P, P], BF16)
        iota8 = sb("iota8", [P, NQ, NE])
        half = sb("half", [P, NQ])
        redo = sb("redo", [1, 1], I32)
        s_redo = sem("first_pass_judged")
        onehot = sb("onehot", [P, 2, NTT, NE], BF16)

        def attention(shifted):
            again = "_shifted" if shifted else ""
            with ExitStack() as es1:
                def sb1(name, shape, dt=F32):
                    return es1.enter_context(nc.sbuf_tensor(name + again, shape, dt))

                def sem1(name):
                    return es1.enter_context(nc.semaphore(name + again))

                sc = es1.enter_context(nc.psum_tensor("scores" + again, [P, 3, 2 * MM], F32))
                po = es1.enter_context(nc.psum_tensor("attn_out" + again, [P, MM], F32))
                pm = es1.enter_context(nc.psum_tensor("spare" + again, [P, MM], F32))
                wq_in = sb1("wq_in", [P, ND, D])
                wk_in = sb1("wk_in", [P, D])
                wv_in = sb1("wv_in", [P, D])
                wo_in = sb1("wo_in", [P, G // 2, D])
                wq = sb1("wq", [P, 2, ND, D])
                wk = sb1("wk", [P, 2, D])
                wv = sb1("wv", [P, 2, D])
                wo = sb1("wo", [P, 2, G // 2, D])
                wg = sb1("wg", [P, ND, NE])
                bqc = sb1("bqc", [P, ND])
                bkc = sb1("bkc", [P, ND])
                bvb = sb1("bvb", [P, D])
                bob = sb1("bob", [P, D])
                x_sb = sb1("x_sb", [P, NQ, D])
                xT = sb1("xT", [P, 2, ND, LQ])
                cT = sb1("cT", [P, 2, LK + 1])
                q_hl = sb1("q_hl", [P, 2, ND, LQ])
                k_hl = sb1("k_hl", [P, 2, ND, LK + 1])
                q_st = sb1("q_st", [P, 2 * HG, LQ])
                k_st = sb1("k_st", [P, HG, LK + 1])
                v_raw = sb1("v_raw", [P, NT, D])
                c_sb = v_raw[:, 0:(NT * DC + D - 1) // D, :].rearrange("p t d -> p (t d)")[:, 0:NT * DC].rearrange(
                    "p (t d) -> p t d", d=DC)
                VW = DH + 1
                v_st = sb1("v_st", [P, NT, H * VW + DH])
                pr = sb1("probs", [P, 2, 2, 2 * MM])
                o_t = sb1("o_t", [P, NB32, 32])
                o_n = sb1("o_n", [P, NB32, 32])
                rec = sb1("rec", [P, NB32])
                rok = sb1("rok", [P, NB32])
                at = sb1("attnT", [P, 2, G // 2, LQ])
                x1 = sb1("x1", [P, NQ, D])
                xn2 = sb1("xn2", [P, NQ, XW])
                nT = sb1("nT", [P, ND, LQ])
                st1 = sb1("st1", [P, NQ, 6])
                mv1 = sb1("mv1", [P, NQ, 2])
                rstd1 = sb1("rstd1", [P, NQ])
                st2 = sb1("st2", [P, NQ, 6])
                mv2 = sb1("mv2", [P, NQ, 2])
                rstd2 = sb1("rstd2", [P, NQ])
                lg = sb1("lg", [P, NQ, NE])
                mx = sb1("mx", [P, NQ, NE])
                mi = sb1("mi", [P, NQ, NE], U32)
                mif = sb1("mif", [P, NQ, 2])
                zz = sb1("zz", [P, NQ, NE])
                ez = sb1("ez", [P, NQ, NE])
                gs = sb1("gs", [P, NQ])
                oh = sb1("oh", [P, 2, NQ, NE])
                if shifted:
                    KM = HG * NQ
                    zrow = sb1("zrow", [2, LQ])
                    mxv = sb1("mxv", [P, KM])
                    mrow = sb1("mrow", [KM, 2, P])
                    s_mr = sem1("unshifted_scores_ready")
                    s_md = sem1("maxima_taken")
                    s_ms = sem1("shift_rows_filled")
                    sflat = sc[:, :, :].rearrange("p a b -> p (a b)")
                else:
                    red = sb1("red", [P, 2, B * G])
                    okc = sb1("okc", [P, 1])
                    onec = sb1("onec", [P, 1])

                s_const = sem1("consts_made")
                s_w = sem1("weights_loaded")
                s_w2 = sem1("late_weights_loaded")
                s_ws = sem1("weights_split")
                s_x = sem1("x_loaded")
                s_c = sem1("ctx_loaded")
                s_xr = sem1("residual_loaded")
                s_st = [sem1(f"stacks_filled{g}") for g in range(G)]
                s_sc = sem1("scores_ready")
                s_exp = sem1("probs_ready")
                s_pv = sem1("pv_done")
                s_oc = sem1("attn_out_copied")
                s_prep = sem1("prep_item_ready")
                s_prepd = sem1("prep_item_taken")
                s_epi = sem1("epi_item_ready")
                s_epid = sem1("epi_item_taken")
                s_v = sem1("v_group_placed")
                s_mv1 = sem1("ln1_stats_ready")
                s_r1 = sem1("ln1_rstd_ready")
                s_mv2 = sem1("ln2_stats_ready")
                s_r2 = sem1("ln2_rstd_ready")
                s_bo = sem1("residual_biased")
                s_z = sem1("gate_logits_shifted")
                s_ez = sem1("gate_exp_ready")
                s_n = sem1("ln2_rows_ready")
                s_nx = sem1("routed_rows_ready")
                s_at = sem1("attnT_ready")
                s_xn = sem1("ln1_rows_ready")
                s_x1o = sem1("x1_stored")
                s_xno = sem1("routed_rows_stored")
                s_ok = sem1("verdict_per_partition")
                s_okp = sem1("verdict_summed")
                s_past = sem1("dve_waits_passed")
                s_past_p = sem1("pool_waits_passed")
                s_past_sp = sem1("sp_waits_passed")
                s_dve = sem1("dve_step")

                block = es1.enter_context(nc.Block())

                def program(engine):
                    def declare(steps):
                        @engine
                        def _(eng):
                            if not shifted:
                                steps(eng)
                            else:
                                eng.wait_ge(s_redo, 1)
                                with eng.If(eng.value_load(redo[0:1, 0:1], min_val=0, max_val=P)):
                                    steps(eng)
                    return declare

                NCONST = 15
                NW = 16 * (ND + 2 + 3)
                NW2 = 16 * (2 + 2 * HG)

                def slot(h):
                    return h % (2 * HG)

                def pair(h):
                    return h // 2 % HG

                STK = 16 * HG * (7 if shifted else 6)

                @program(block.sync)
                def _(sp):
                    sp.dma_start(x_sb[:, :, :], x[0].rearrange("(t p) d -> p t d", p=P)).then_inc(s_x, 16)
                    sp.dma_start(c_sb[:, 0:NT - 1, :],
                                 ctx[0, 0:(NT - 1) * P].rearrange("(t p) d -> p t d", p=P)).then_inc(s_c, 16)
                    sp.dma_start(c_sb[0:LAST, NT - 1, :], ctx[0, (NT - 1) * P:LK]).then_inc(s_c, 16)
                    for c in range(ND):
                        sp.dma_start(wq_in[:, c, :], Wq[c * P:(c + 1) * P, :]).then_inc(s_w, 16)
                    sp.dma_start(wk_in[:, :], Wk).then_inc(s_w, 16)
                    with nc.allow_non_contiguous_dma(reason="bias columns, once"):
                        sp.dma_start(bqc[:, :], bq.rearrange("(c p) -> p c", p=P)).then_inc(s_w, 16)
                        sp.dma_start(bkc[:, :], bk.rearrange("(c p) -> p c", p=P)).then_inc(s_w, 16)
                    sp.dma_start(wv_in[:, :], Wv).then_inc(s_w, 16)
                    sp.dma_start(bvb[:, :], bv.rearrange("(a n) -> a n", a=1).broadcast_to([P, D])).then_inc(s_w, 16)

                    def late_weights():
                        with nc.allow_non_contiguous_dma(reason="gate weights, once"):
                            sp.dma_start(wg[:, :, :], w_gate.rearrange("(c p) e -> p c e", p=P)).then_inc(s_w2, 16)
                        sp.dma_start(bob[:, :], bo.rearrange("(a n) -> a n", a=1).broadcast_to([P, D])).then_inc(s_w2, 16)
                        wo_v = Wo.rearrange("(p i h d) n -> h i d p n", i=2, h=HG, d=DH)
                        for h in range(HG):
                            for i in range(2):
                                row = 32 * h + DH * i
                                sp.dma_start(wo_in[row:row + DH, :, :], wo_v[h, i]).then_inc(s_w2, 16)

                    def stacks(b, g):
                        sp.wait_ge(s_prepd, b * NP + (V_k if g < GC else NP))
                        stand(sp, s_past_sp)
                        if g >= 2:
                            sp.wait_ge(s_sc, b * 2 * STEPS + 2 * NT * (g - 1))
                        elif not (isinstance(b, int) and b == 0):
                            sp.wait_ge(s_sc, b * 2 * STEPS - 2 * STEPS + 2 * NT * (G + g - 1))
                        for h in range(HG * g, HG * g + HG):
                            c, row, at0 = h * DH // P, h * DH % P, 64 * (h % 2)
                            for k, part in enumerate((0, 1, 0)):
                                sp.dma_start(q_st[at0 + DH * k:at0 + DH * (k + 1), slot(h), :],
                                             q_hl[row:row + DH, part, c, :]).then_inc(s_st[g], 16)
                            for k, part in enumerate((0, 0, 1)):
                                sp.dma_start(k_st[at0 + DH * k:at0 + DH * (k + 1), pair(h), :],
                                             k_hl[row:row + DH, part, c, :]).then_inc(s_st[g], 16)
                            if shifted:
                                sp.dma_start(q_st[at0 + 3 * DH:at0 + 3 * DH + 2, slot(h), :], zrow[:, :]).then_inc(s_st[g], 16)

                    sp.wait_ge(s_const, NCONST)
                    stacks(0, 0)
                    late_weights()
                    stacks(0, 1)

                    def store_x1(b):
                        rows = out_rows[bass.ds(b * LQ, LQ), :].rearrange("(t p) d -> p t d", p=P)
                        sp.wait_ge(s_epid, b * NEP + nT_k)
                        sp.dma_start(rows, x1[:, :, :]).then_inc(s_x1o, 16)

                    def store_rows(b):
                        rows = xn2_dram[bass.ds(b * LQ, LQ), :].rearrange("(t p) d -> p t d", p=P)
                        sp.wait_ge(s_nx, b + 1)
                        sp.dma_start(rows, xn2[:, :, :]).then_inc(s_xno, 16)

                    def body(b, first, final):
                        if not final:
                            sp.wait_ge(s_prep, b * NP + ND)
                            sp.dma_start(x_sb[:, :, :],
                                         x[bass.ds(b + 1, 1)].rearrange("o (t p) d -> p (o t) d", p=P)).then_inc(s_x, 16)
                        if not first:
                            stacks(b, 1)
                        if not final:
                            sp.wait_ge(s_v, b * G + G)
                            sp.dma_start(c_sb[:, 0:NT - 1, :],
                                         ctx[bass.ds(b + 1, 1), 0:(NT - 1) * P].rearrange("o (t p) d -> p (o t) d", p=P)).then_inc(s_c, 16)
                            sp.dma_start(c_sb[0:LAST, NT - 1, :],
                                         ctx[bass.ds(b + 1, 1), (NT - 1) * P:LK].rearrange("o p d -> p (o d)")).then_inc(s_c, 16)
                        if not first:
                            store_x1(b - 1)
                        stacks(b, 2)
                        if not first:
                            store_rows(b - 1)
                            sp.wait_ge(s_x1o, 16 * b)
                            sp.wait_ge(s_xno, 16 * b)
                        sp.dma_start(x1[:, :, :], x[bass.ds(b, 1)].rearrange("o (t p) d -> p (o t) d", p=P)).then_inc(s_xr, 16)
                        stacks(b, 3)
                        if not final:
                            stacks(b + 1, 0)

                    body(0, True, False)
                    with sp.Fori(1, B - 1) as b:
                        body(b, False, False)
                    body(B - 1, False, True)
                    store_x1(B - 1)
                    store_rows(B - 1)
                    sp.wait_ge(s_x1o, 16 * B)
                    sp.wait_ge(s_xno, 16 * B)

                @program(block.gpsimd)
                def _(pool):
                    pool.memset(ident[:, :], 0.0).then_inc(s_const, 1)
                    pool.memset(tri[:, :], 1.0).then_inc(s_const, 1)
                    pool.memset(ones_b[:, :], 1.0).then_inc(s_const, 1)
                    pool.memset(half[:, :], -0.5).then_inc(s_const, 1)
                    pool.memset(v_raw[:, NT - 1, :], 0.0).then_inc(s_const, 1)
                    pool.memset(k_hl[:, :, :, LK:LK + 1], 0.0).then_inc(s_const, 1)
                    pool.memset(cT[:, :, LK:LK + 1], 0.0).then_inc(s_const, 1)
                    heads = v_st[:, :, 0:H * VW].rearrange("p t (h c) -> p t h c", h=H)
                    pool.memset(heads[:, :, :, DH:VW], 1.0).then_inc(s_const, 1)
                    pool.memset(v_st[:, :, H * VW:], 1.0).then_inc(s_const, 1)
                    pool.iota(iota8[:, :, :], [[0, NQ], [1, NE]], base=0, channel_multiplier=0,
                              allow_small_or_imprecise_dtypes=True).then_inc(s_const, 1)
                    pool.wait_ge(s_const, 11)
                    pool.affine_select(out=ident[:, :], in_=ident[:, :], compare_op=ALU.not_equal, fill=1.0,
                                       base=0, pattern=[[-1, P]], channel_multiplier=1).then_inc(s_const, 1)
                    pool.affine_select(out=tri[:, :], in_=tri[:, :], compare_op=ALU.is_gt, fill=0.0,
                                       base=0, pattern=[[1, P]], channel_multiplier=-1).then_inc(s_const, 1)
                    pool.memset(q_st[:, :, :], 0.0).then_inc(s_const, 1)
                    if shifted:
                        pool.memset(zrow[:, :], 0.0).then_inc(s_const, 1)
                    else:
                        pool.memset(onec[:, :], 1.0).then_inc(s_const, 1)

                    def ln1(b):
                        pool.wait_ge(s_mv1, b + 1)
                        pool.tensor_tensor(rstd1[:, :], mv1[:, :, 1], half[:, :], ALU.pow).then_inc(s_r1, 1)

                    def place(b, g):
                        if not (isinstance(b, int) and b == 0):
                            pool.wait_ge(s_pv, b * STEPS - STEPS + NT * (g + 1))
                        stand(pool, s_past_p)
                        w = slice(HG * g * VW, HG * (g + 1) * VW)
                        dst = v_st[:, :, w].rearrange("p t (h c) -> p t h c", h=HG)[:, :, :, 0:DH]
                        src = v_raw[:, :, HG * g * DH:HG * (g + 1) * DH].rearrange("p t (h c) -> p t h c", h=HG)
                        for t in range(NT):
                            ins = pool.tensor_copy(dst[:, t], src[:, t])
                        ins.then_inc(s_v, 1)

                    def ln2(b):
                        pool.wait_ge(s_xr, 16 * b + 16)
                        for t in range(NQ):
                            ins = pool.tensor_tensor(x1[:, t, :], x1[:, t, :], bob[:, :], ALU.add)
                        ins.then_inc(s_bo, 1)
                        pool.wait_ge(s_mv2, b + 1)
                        pool.tensor_tensor(rstd2[:, :], mv2[:, :, 1], half[:, :], ALU.pow).then_inc(s_r2, 1)

                    pool.wait_ge(s_const, NCONST)
                    ln1(0)
                    pool.wait_ge(s_prepd, V_k + NT)
                    for g in range(G):
                        place(0, g)

                    def body(b, first, final):
                        if not first:
                            ln2(b - 1)
                        if not final:
                            ln1(b + 1)
                            pool.wait_ge(s_prepd, (b + 1) * NP + V_k + NT)
                            for g in range(G):
                                place(b + 1, g)

                    pool.wait_ge(s_w2, NW2)
                    body(0, True, False)
                    with pool.Fori(1, B - 1) as b:
                        body(b, False, False)
                    body(B - 1, False, True)
                    ln2(B - 1)

                @program(block.scalar)
                def _(act):
                    def body(b, first):
                        for n in range(2 * STEPS):
                            u, j = n // 2, n % 2
                            if shifted and n % (2 * NT) == 0:
                                shift_rows(b, u // NT)
                            rows = P if u % NT < NT - 1 else LAST
                            act.wait_ge(s_sc, b * 2 * STEPS + n + 1)
                            if not (first and u < 2):
                                act.wait_ge(s_pv, b * STEPS + u - 1)
                            act.activation(pr[0:rows, u % 2, j, :], sc[0:rows, BANK[n], :], ACT.Exp,
                                           scale=SCALE).then_inc(s_exp, 1)
                            if n == 2 * GATE_EXP and not first:
                                gate(b - 1)

                    def shift_rows(b, g):
                        act.wait_ge(s_md, (b * G + g + 1) * (KM + 1))
                        for k in range(KM):
                            h = HG * g + k // NQ
                            row, cols = 64 * (h % 2) + 3 * DH, slice(k % NQ * P, (k % NQ + 1) * P)
                            for part in range(2):
                                act.dma_start(q_st[row + part:row + part + 1, slot(h), cols],
                                              mrow[k:k + 1, part, :]).then_inc(s_ms, 16)

                    def gate(b):
                        act.wait_ge(s_z, b + 1)
                        act.activation(ez[:, :, :], zz[:, :, :], ACT.Exp).then_inc(s_ez, 1)

                    body(0, True)
                    with act.Fori(1, B) as b:
                        body(b, False)
                    gate(B - 1)

                @program(block.tensor)
                def _(pe):
                    def product(bank, factors):
                        terms = [(lhsT, rhs, i, j) for lhsT, rhs in factors for i, j in HALVES]
                        for n, (lhsT, rhs, i, j) in enumerate(terms):
                            ins = pe.matmul(bank, r(lhsT[:, i]), r(rhs[:, j]), start=(n == 0), stop=(n == len(terms) - 1))
                        return ins

                    def prep(b, k):
                        project_q(b, k, range(ND)) if PREP[k][0] == "Q" else prep_other(b, k)

                    def project_q(b, k, chunks):
                        c = PREP[k][1]
                        for k2 in chunks:
                            for i, j in HALVES:
                                ins = pe.matmul(pm[:, 0:LQ], r(wq[:, i, k2, c * P:(c + 1) * P]), r(xT[:, j, k2, :]),
                                                start=(k2 == 0 and i + j == 0),
                                                stop=(k2 == ND - 1 and (i, j) == HALVES[-1]))
                        if k2 == ND - 1:
                            ins.then_inc(s_prep, 1)

                    def prep_other(b, k):
                        kind, *arg = PREP[k]
                        if kind == "xT":
                            c, = arg
                            if c == 0:
                                pe.wait_ge(s_xn, b + 1)
                            for t in range(NQ):
                                ins = pe.transpose(pm[:, t * P:(t + 1) * P], x_sb[:, t, c * P:(c + 1) * P], ident[:, :])
                        elif kind == "cT":
                            n, = arg
                            if n == 0:
                                pe.wait_ge(s_c, b * 32 + 32)
                            for t in range(4 * n, min(4 * n + 4, NT)):
                                w = P if t < NT - 1 else LAST
                                ins = pe.transpose(pm[:, (t - 4 * n) * P:(t - 4 * n) * P + w], c_sb[0:w, t, :],
                                                   ident[0:w, 0:w])
                        elif kind == "K":
                            c, n = arg
                            w = min(MM, LK + LK % 2 - n * MM)
                            ins = product(pm[:, 0:w], [(wk[:, :, c * P:(c + 1) * P], cT[:, :, n * MM:n * MM + w])])
                        else:
                            n, = arg
                            w = P if n < NT - 1 else LAST
                            ins = product(pm[0:w, 0:D], [(cT[:, :, n * P:n * P + w], wv[:, :, :])])
                        ins.then_inc(s_prep, 1)

                    def epi(b, k):
                        kind, *arg = EPI[k]
                        if kind == "O":
                            n, = arg
                            if n == 0:
                                pe.wait_ge(s_ws, 4)
                                pe.wait_ge(s_at, b * (G // 2) + G // 2)
                            ins = product(pm[:, 0:D], [(at[:, :, p2, n * P:(n + 1) * P], wo[:, :, p2, :])
                                                       for p2 in range(G // 2)])
                        elif kind == "nT":
                            c, = arg
                            if c == 0:
                                pe.wait_ge(s_n, b + 1)
                            for t in range(NQ):
                                ins = pe.transpose(pm[:, t * P:(t + 1) * P], xn2[:, t, c * P:(c + 1) * P], ident[:, :])
                        else:
                            t, = arg
                            for c in range(ND):
                                ins = pe.matmul(pm[:, 0:NE], nT[:, c, t * P:(t + 1) * P], wg[:, c, :],
                                                start=(c == 0), stop=(c == ND - 1))
                        ins.then_inc(s_epi, 1)

                    def pv(b, u, first):
                        g, t = u // NT, u % NT
                        rows = P if t < NT - 1 else LAST
                        pe.wait_ge(s_exp, b * 2 * STEPS + 2 * u + 2)
                        if t == 0:
                            pe.wait_ge(s_v, b * G + min(g + 2, G))
                            if not (first and g == 0):
                                pe.wait_ge(s_oc, b * G + g)
                        for h in range(HG):
                            c = (HG * g + h) * VW
                            ins = pe.matmul(po[32 * h:32 * h + 32, 0:LQ], v_st[0:rows, t, c:c + 32],
                                            pr[0:rows, u % 2, h // 2, (h % 2) * LQ:(h % 2 + 1) * LQ],
                                            start=(t == 0), stop=(t == NT - 1), tile_position=(0, 32 * h))
                        ins.then_inc(s_pv, 1)

                    def maxima(b, g, u, first):
                        if u > 0 or not first:
                            pe.wait_ge(s_exp, b * 2 * STEPS + 2 * u)
                        done = (b * G + g) * (KM + 1)
                        for k in range(KM):
                            h = HG * g + k // NQ
                            if k > 0:
                                pe.wait_ge(s_md, done + k)
                            for n in range(NKC):
                                w = min(MM, LK + LK % 2 - n * MM)
                                ins = pe.matmul(sflat[:, n * MM:n * MM + w],
                                                r(q_st[:, slot(h), k % NQ * P:(k % NQ + 1) * P]),
                                                r(k_st[:, pair(h), n * MM:n * MM + w]), start=True, stop=True)
                            ins.then_inc(s_mr, 1)
                        pe.wait_ge(s_md, done + KM)
                        pe.transpose(sflat[0:KM, 5 * MM:5 * MM + P], mxv[:, :], ident[:, :]).then_inc(s_mr, 1)
                        pe.wait_ge(s_ms, (b * G + g + 1) * KM * 2 * 16)
                        pe.wait_ge(s_md, done + KM + 1)

                    def body(b, first, final):
                        for u in range(STEPS):
                            g, t = u // NT, u % NT
                            if t == 0:
                                pe.wait_ge(s_st[g], b * STK + STK)
                                if shifted:
                                    maxima(b, g, u, first)
                            rows = P if t < NT - 1 else LAST
                            for j in range(2):
                                n = 2 * u + j
                                before = [m for m in range(n) if BANK[m] == BANK[n]]
                                if before:
                                    pe.wait_ge(s_exp, b * 2 * STEPS + before[-1] + 1)
                                elif not first:
                                    before = max(m for m in range(2 * STEPS) if BANK[m] == BANK[n])
                                    pe.wait_ge(s_exp, b * 2 * STEPS - 2 * STEPS + before + 1)
                                for h in (HG * g + 2 * j, HG * g + 2 * j + 1):
                                    ins = pe.matmul(sc[0:rows, BANK[n], (h % 2) * MM:(h % 2) * MM + LQ],
                                                    r(k_st[:, pair(h), t * P:t * P + rows]), r(q_st[:, slot(h), :]),
                                                    start=True, stop=True)
                                ins.then_inc(s_sc, 1)
                            if u > 0:
                                pv(b, u - 1, first)
                            elif not first:
                                pv(b - 1, STEPS - 1, False)
                            if u in late and not first:
                                if late[u] == 0:
                                    pe.wait_ge(s_prepd, b * NP + NP)
                                else:
                                    pe.wait_ge(s_epid, (b - 1) * NEP + late[u])
                                epi(b - 1, late[u])
                            if first and u in start_at:
                                pe.wait_ge(s_prepd, start_at[u])
                                prep(0, start_at[u])
                            if u in prep_at and not final:
                                k = prep_at[u]
                                if k == 0 and not first:
                                    pe.wait_ge(s_epid, b * NEP)
                                pe.wait_ge(s_prepd, (b + 1) * NP + k)
                                if PREP[k][0] == "Q":
                                    project_q(b + 1, k, range(ND - 1, ND))
                                else:
                                    prep(b + 1, k)
                            if u in q_half and not final:
                                k, h = q_half[u]
                                pe.wait_ge(s_prepd, (b + 1) * NP + k)
                                project_q(b + 1, k, range(h, h + 1))

                    pe.wait_ge(s_const, NCONST)
                    pe.wait_ge(s_w, NW)
                    pe.wait_ge(s_ws, 3)
                    for k in range(V_k + NT):
                        if k:
                            pe.wait_ge(s_prepd, k)
                        prep(0, k)
                    body(0, True, False)
                    with pe.Fori(1, B - 1) as b:
                        body(b, False, False)
                    body(B - 1, False, True)
                    pv(B - 1, STEPS - 1, False)
                    for k in range(NEP):
                        pe.wait_ge(s_epid, (B - 1) * NEP + k)
                        epi(B - 1, k)
                    if not shifted:
                        pe.wait_ge(s_epid, (B - 1) * NEP + NEP)
                        pe.wait_ge(s_ok, 1)
                        pe.matmul(pm[0:1, 0:1], okc[:, 0:1], onec[:, :], start=True, stop=True).then_inc(s_okp, 1)

                @program(block.vector)
                def _(dve):
                    chained = [0]

                    counted = [0]
                    links = LINKS + (G if shifted else 3 * G + 2)

                    def link(ins):
                        ins.then_inc(s_dve, 1)
                        chained[0] = chained[0] + 1
                        counted[0] += 1
                        dve.wait_ge(s_dve, chained[0])

                    def stats(src, t, st):
                        return dve.bn_stats(st[:, t, :], src[:, t, :])

                    def moments(st, mv, signal):
                        stand(dve, s_past)
                        for t in range(NQ):
                            ins = dve.bn_aggr(mv[:, t, :], st[:, t, :])
                        link(ins)
                        dve.tensor_scalar(mv[:, :, 1], mv[:, :, 1], EPS, None, ALU.add).then_inc(signal, 1)

                    def ln1_stats(b):
                        dve.wait_ge(s_x, b * 16 + 16)
                        for t in range(NQ):
                            ins = stats(x_sb, t, st1)
                        link(ins)
                        moments(st1, mv1, s_mv1)

                    def ln1_apply(b):
                        dve.wait_ge(s_mv1, b + 1)
                        dve.wait_ge(s_r1, b + 1)
                        for t in range(NQ):
                            ins = dve.tensor_scalar(x_sb[:, t, :], x_sb[:, t, :], mv1[:, t, 0:1], rstd1[:, t:t + 1],
                                                    ALU.subtract, ALU.mult)
                        ins.then_inc(s_xn, 1)

                    def split(bank, bias, hi, lo):
                        link(dve.tensor_scalar(r(hi), bank, bias, None, ALU.add))
                        dve.scalar_tensor_tensor(r(lo), bank, bias, hi, ALU.add, ALU.subtract).then_inc(s_prepd, 1)

                    def in_halves(whole, hi, lo, signal):
                        link(dve.tensor_copy(r(hi), whole))
                        dve.tensor_tensor(r(lo), whole, hi, ALU.subtract).then_inc(signal, 1)

                    def prep(b, k):
                        kind, *arg = PREP[k]
                        dve.wait_ge(s_prep, b * NP + k + 1)
                        if kind == "xT":
                            in_halves(pm[:, 0:LQ], xT[:, 0, arg[0], :], xT[:, 1, arg[0], :], s_prepd)
                        elif kind == "Q":
                            c, = arg
                            if not (isinstance(b, int) and b == 0):
                                for g in range(GC * c, GC * (c + 1)):
                                    dve.wait_ge(s_st[g], b * STK)
                            split(pm[:, 0:LQ], bqc[:, c:c + 1], q_hl[:, 0, c, :], q_hl[:, 1, c, :])
                        elif kind == "cT":
                            n, = arg
                            w = min(MM, LK - n * MM)
                            in_halves(pm[:, 0:w], cT[:, 0, n * MM:n * MM + w], cT[:, 1, n * MM:n * MM + w], s_prepd)
                        elif kind == "K":
                            c, n = arg
                            w = min(MM, LK - n * MM)
                            at0 = slice(n * MM, n * MM + w)
                            split(pm[:, 0:w], bkc[:, c:c + 1], k_hl[:, 0, c, at0], k_hl[:, 1, c, at0])
                        else:
                            n, = arg
                            if n == 0 and not (isinstance(b, int) and b == 0):
                                dve.wait_ge(s_v, b * G)
                            w = P if n < NT - 1 else LAST
                            dve.tensor_tensor(v_raw[0:w, n, :], pm[0:w, 0:D], bvb[0:w, :], ALU.add).then_inc(s_prepd, 1)

                    def leave(b, g):
                        dve.wait_ge(s_pv, b * STEPS + NT * (g + 1))
                        dve.transpose(o_t[:, :, :].rearrange("p a c -> p (a c)"), po[:, 0:LQ]).then_inc(s_oc, 1)

                    def divide(b, g):
                        dve.wait_ge(s_oc, b * G + g + 1)
                        link(dve.reciprocal(rec[:, :], o_t[:, :, DH]))
                        i = g % 2
                        link(dve.tensor_tensor(o_n[:, :, DH * i:DH * (i + 1)], o_t[:, :, 0:DH],
                                               rec[:, :].rearrange("p (a o) -> p a o", o=1).broadcast_to([P, NB32, DH]),
                                               ALU.mult))

                    def turn_back(b, g):
                        if g % 2 == 1:
                            turned = o_t[:, :, :].rearrange("p a c -> p (a c)")
                            link(dve.transpose(turned, o_n[:, :, :].rearrange("p a c -> p (a c)")))
                            in_halves(turned, at[:, 0, g // 2, :], at[:, 1, g // 2, :], s_at)
                            dve.wait_ge(s_at, b * (G // 2) + g // 2 + 1)

                    def judge(b, g):
                        if not shifted:
                            link(dve.tensor_scalar(rok[:, :], rec[:, :], SUM_REACH, None, ALU.is_lt))
                            link(dve.scalar_tensor_tensor(rok[:, :], rec[:, :], 1.0 / SUM_REACH, rok[:, :],
                                                          ALU.is_gt, ALU.mult))
                            link(dve.tensor_reduce(red[:, 0, bass.ds(b * G + g, 1)], rok[:, :], AX.X, ALU.min,
                                                   negate=True))

                    def finite(b):
                        link(dve.tensor_scalar(rok[:, 0:NQ], mv2[:, :, 1], OUT_REACH, None, ALU.is_lt))
                        link(dve.tensor_reduce(red[:, 1, bass.ds(b * G, 1)], rok[:, 0:NQ], AX.X, ALU.min, negate=True))

                    def verdict():
                        link(dve.tensor_reduce(okc[:, 0:1], red[:, :, :], AX.XY, ALU.max))
                        dve.tensor_scalar(okc[:, 0:1], okc[:, 0:1], -0.5, None, ALU.is_gt).then_inc(s_ok, 1)
                        dve.wait_ge(s_okp, 1)
                        dve.tensor_copy(redo[0:1, 0:1], pm[0:1, 0:1]).then_inc(s_redo, 1)

                    def maxima(b, g):
                        done = (b * G + g) * (KM + 1)
                        for k in range(KM):
                            dve.wait_ge(s_mr, done + k + 1)
                            dve.tensor_reduce(mxv[:, k:k + 1], sflat[:, 0:LK], AX.X, ALU.max).then_inc(s_md, 1)
                        dve.wait_ge(s_mr, done + KM + 1)
                        bank = sflat[0:KM, 5 * MM:5 * MM + P]
                        link(dve.tensor_scalar(r(mrow[:, 0, :]), bank, -1.0, None, ALU.mult))
                        dve.scalar_tensor_tensor(r(mrow[:, 1, :]), bank, -1.0, mrow[:, 0, :], ALU.mult,
                                                 ALU.subtract).then_inc(s_md, 1)

                    def epi(b, k):
                        kind, *arg = EPI[k]
                        dve.wait_ge(s_epi, b * NEP + k + 1)
                        if kind == "O":
                            n, = arg
                            if n == 0:
                                dve.wait_ge(s_bo, b + 1)
                            dve.tensor_tensor(x1[:, n, :], pm[:, 0:D], x1[:, n, :], ALU.add).then_inc(s_epid, 1)
                            dve.wait_ge(s_epid, b * NEP + k + 1)
                            link(stats(x1, n, st2))
                            if n == NQ - 1:
                                moments(st2, mv2, s_mv2)
                        elif kind == "nT":
                            dve.tensor_copy(nT[:, arg[0], :], pm[:, 0:LQ]).then_inc(s_epid, 1)
                        else:
                            t, = arg
                            dve.tensor_copy(lg[:, t, :], pm[:, 0:NE]).then_inc(s_epid, 1)
                            if t == NQ - 1:
                                gate(b, k)

                    def ln2_apply(b):
                        dve.wait_ge(s_mv2, b + 1)
                        if not shifted:
                            finite(b)
                        dve.wait_ge(s_r2, b + 1)
                        for t in range(NQ):
                            ins = dve.tensor_scalar(xn2[:, t, 0:D], x1[:, t, :], mv2[:, t, 0:1], rstd2[:, t:t + 1],
                                                    ALU.subtract, ALU.mult)
                        ins.then_inc(s_n, 1)

                    def gate(b, k):
                        dve.wait_ge(s_epid, b * NEP + k + 1)
                        stand(dve, s_past)
                        for t in range(NQ):
                            ins = dve.max(mx[:, t, :], lg[:, t, :])
                        link(ins)
                        dve.tensor_tensor(zz[:, :, :], lg[:, :, :], mx[:, :, 0:1].broadcast_to([P, NQ, NE]),
                                          ALU.subtract).then_inc(s_z, 1)
                        for t in range(NQ):
                            ins = dve.max_index(mi[:, t, :], mx[:, t, :], lg[:, t, :])
                        link(ins)
                        link(dve.tensor_copy(mif[:, :, :], mi[:, :, 0:2]))
                        for k2 in range(2):
                            ins = dve.tensor_tensor(oh[:, k2, :, :], iota8[:, :, :],
                                                    mif[:, :, k2:k2 + 1].broadcast_to([P, NQ, NE]), ALU.is_equal)
                        link(ins)

                    def gates(b):
                        dve.wait_ge(s_ez, b + 1)
                        link(dve.tensor_reduce(gs[:, :], ez[:, :, :], AX.X, ALU.add))
                        link(dve.reciprocal(gs[:, :], gs[:, :]))
                        link(dve.tensor_tensor(ez[:, :, :], ez[:, :, :],
                                               gs[:, :].rearrange("p (t o) -> p t o", o=1).broadcast_to([P, NQ, NE]), ALU.mult))
                        link(dve.tensor_tensor(lg[:, :, :], oh[:, 0, :, :], oh[:, 1, :, :], ALU.add))
                        dve.tensor_tensor(xn2[:, :, D:XW], ez[:, :, :], lg[:, :, :], ALU.mult).then_inc(s_nx, 1)
                        link(dve.tensor_copy(onehot[:, :, bass.ds(b * NQ, NQ), :], oh[:, :, :, :]))

                    def body(b, first, final):
                        for u in range(STEPS):
                            if shifted and u % NT == 0:
                                maxima(b, u // NT)
                            group_done = (b, u // NT - 1) if u >= NT else None if first else (b - 1, G - 1)
                            if u % NT == 0 and group_done:
                                leave(*group_done)
                            if u in late and not first:
                                epi(b - 1, late[u])
                            if first and u in start_at:
                                prep(0, start_at[u])
                            if u in prep_at and not final:
                                prep(b + 1, prep_at[u])
                            for step, work in enumerate((divide, turn_back, judge)):
                                if u % NT == 1 + step and group_done:
                                    work(*group_done)
                            if u == 8 and not first:
                                ln2_apply(b - 1)
                            if u == LN1_STATS and not final:
                                ln1_stats(b + 1)
                            if u == GATE_END and not first:
                                gates(b - 1)
                            if u == LN1_APPLY and not final:
                                ln1_apply(b + 1)

                    dve.memset(k_st[:, :, :], 1.0).then_inc(s_const, 1)
                    if not shifted:
                        link(dve.memset(red[:, :, :], -1.0))
                    ln1_stats(0)
                    dve.wait_ge(s_w, NW)
                    in_halves(wq_in[:, :, :], wq[:, 0], wq[:, 1], s_ws)
                    in_halves(wk_in[:, :], wk[:, 0], wk[:, 1], s_ws)
                    in_halves(wv_in[:, :], wv[:, 0], wv[:, 1], s_ws)
                    ln1_apply(0)
                    for k in range(V_k + NT):
                        prep(0, k)
                    dve.wait_ge(s_w2, NW2)
                    in_halves(wo_in[:, :, :], wo[:, 0], wo[:, 1], s_ws)
                    body(0, True, False)
                    start = chained[0]
                    with dve.Fori(1, B - 1) as b:
                        chained[0] = (b - 1) * links + start
                        counted[0] = 0
                        body(b, False, False)
                        assert counted[0] == links, counted[0]
                    chained[0] = (B - 2) * links + start
                    body(B - 1, False, True)
                    leave(B - 1, G - 1)
                    divide(B - 1, G - 1)
                    turn_back(B - 1, G - 1)
                    judge(B - 1, G - 1)
                    for k in range(NEP):
                        epi(B - 1, k)
                        if k == O_k + NQ - 1:
                            ln2_apply(B - 1)
                    gates(B - 1)
                    if not shifted:
                        verdict()

        attention(False)
        attention(True)

        NSL = CAPACITY // P
        NPAIR = 2 * NTT
        CH = min(16, NTT & -NTT)
        NCH = NPAIR // CH
        COLS = NE * NSL
        with ExitStack() as es2:
            def sb2(name, shape, dt=F32):
                return es2.enter_context(nc.sbuf_tensor(name, shape, dt))

            def sem2(name):
                return es2.enter_context(nc.semaphore(name))

            iota_a = sb2("iota_a", [P, P])
            iota_t = sb2("iota_t", [P, NTT])
            iota_p = sb2("iota_p", [P, 1])
            iota_e = sb2("iota_e", [P, NTT, NE])
            tot = sb2("tot", [P, NTT, NE])
            inc = sb2("inc", [P, NTT, NE])
            pos = sb2("pos", [P, NTT, NE])
            one = sb2("one", [P, NTT])
            tmp = sb2("tmp", [P, 2, NTT, NE])
            pk = sb2("pk", [P, 2, NTT])
            ek = sb2("ek", [P, 2, NTT])
            pi = sb2("pi", [P, 2, NTT], I32)
            li = sb2("li", [P, 2, NTT], I32)
            af = sb2("af", [P, 2, NTT])
            bf = sb2("bf", [P, 2, NTT])
            A = sb2("A", [P, NPAIR, P], BF16)
            Bq = sb2("Bq", [P, CH, COLS], BF16)
            Bt = sb2("Bt", [P, NPAIR, 2, COLS], BF16)
            tab = sb2("tab", [P, 2, COLS])
            occ = sb2("occ", [P, COLS])
            gidx = sb2("gidx", [P, COLS + NSL], I32)
            sidx = sb2("sidx", [P, COLS], I32)
            gst = sb2("gst", [P, 2, NSL], I32)
            sst = sb2("sst", [P, 2, NSL], I32)
            w1 = sb2("w1", [P, 2, ND, 2 * FF])
            w2 = sb2("w2", [P, 2, NF, D])
            xg = [[sb2(f"xg{i}_{c}", [P, XW]) for c in range(NSL)] for i in range(2)]
            gw = sb2("gw", [P, 2, NSL])
            xt = sb2("xt", [P, 2, ND, CAPACITY])
            sa = sb2("sa", [P, 2, MM])
            ht = sb2("ht", [P, NF, CAPACITY])
            ys = [[sb2(f"y{i}_{c}", [P, D]) for c in range(NSL)] for i in range(2)]

            hp = es2.enter_context(nc.psum_tensor("h_banks", [P, 2, 2, MM], F32))
            tp = es2.enter_context(nc.psum_tensor("t_banks", [P, 2, MM], F32))
            yp = es2.enter_context(nc.psum_tensor("y_banks", [P, 2, MM], F32))

            s_i = sem2("iotas_made")
            s_cum = sem2("counts_ready")
            s_ab = sem2("onehots_ready")
            s_tab = sem2("table_ready")
            s_idx = sem2("indices_ready")
            s_wt = [sem2(f"expert_weights{i}") for i in range(2)]
            s_stg = sem2("gather_indices_staged")
            s_ssg = sem2("scatter_indices_staged")
            s_g = [sem2(f"rows_gathered{i}") for i in range(2)]
            s_t = sem2("rows_transposed")
            s_td = sem2("rows_T_copied")
            s_a = sem2("hidden_ready")
            s_si = sem2("silu_ready")
            s_h = sem2("gated_ready")
            s_y = sem2("y_ready")
            s_ye = sem2("y_scaled")
            s_gw = sem2("gates_ready")
            s_yf = sem2("experts_added")
            s_add = sem2("y_added")
            s_d2 = sem2("dve_step2")
            s_past2 = sem2("pool_waits_passed2")
            block = es2.enter_context(nc.Block())

            H2 = CAPACITY // MM
            UN = H2 * NF
            NTI = H2 * ND

            ORDER = ([("h", k) for k in range(NF + 1)] + [("y", k) for k in range(MM // P)]
                     + [("h", k) for k in range(NF + 1, UN)] + [("t", k) for k in range(NTI)]
                     + [("y", k) for k in range(MM // P, NSL)])

            @block.sync
            def _(sp):
                def load(e, i):
                    sp.dma_start(w1[:, i, :, :],
                                 c_fc[bass.ds(e, 1)].rearrange("o (c p) f -> p (o c) f", p=P)).then_inc(s_wt[i], 16)
                    sp.dma_start(w2[:, i, :, :],
                                 c_proj[bass.ds(e, 1)].rearrange("o (c p) f -> p (o c) f", p=P)).then_inc(s_wt[i], 16)

                load(0, 0)
                load(1, 1)
                with sp.Fori(0, NE // 2 - 1) as pair:
                    e = pair * 2
                    for i in range(2):
                        sp.wait_ge(s_y, (e + i) * NSL + NSL)
                        load(e + i + 2, i)

            @block.gpsimd
            def _(pool):
                pool.iota(iota_a[:, :], [[1, P]], base=0, channel_multiplier=0,
                          allow_small_or_imprecise_dtypes=True).then_inc(s_i, 1)
                pool.iota(iota_t[:, :], [[1, NTT]], base=1, channel_multiplier=0,
                          allow_small_or_imprecise_dtypes=True).then_inc(s_i, 1)
                pool.iota(iota_p[:, :], [[0, 1]], base=0, channel_multiplier=1,
                          allow_small_or_imprecise_dtypes=True).then_inc(s_i, 1)
                pool.iota(iota_e[:, :, :], [[0, NTT], [1, NE]], base=0, channel_multiplier=0,
                          allow_small_or_imprecise_dtypes=True).then_inc(s_i, 1)
                pool.memset(one[:, :], 1.0).then_inc(s_i, 1)
                pool.memset(gidx[:, COLS:], 0).then_inc(s_i, 1)
                def gather(e, i):
                    stand(pool, s_past2)
                    pool.tensor_copy(gst[:, i, :], gidx[:, bass.ds(e * NSL, NSL)]).then_inc(s_stg, 1)
                    pool.wait_ge(s_stg, e + 1)
                    stand(pool, s_past2)
                    for c in range(NSL):
                        pool.indirect_dma_start(out=xg[i][c][:, :], out_offset=None, in_=xn2_dram[:, :],
                                                in_offset=bass.IndirectOffsetOnAxis(ap=gst[:, i, c:c + 1], axis=0),
                                                bounds_check=NTOK - 1, oob_is_err=False).then_inc(s_g[i], 16)

                for c in range(2):
                    pool.sem_inc(s_yf, 1)
                pool.wait_ge(s_idx, 1)
                gather(0, 0)
                with pool.Fori(0, NE // 2) as pair:
                    e2 = pair * 2
                    for i in range(2):
                        e = e2 + i
                        pool.wait_ge(s_t, e * NTI + NTI)
                        pool.wait_ge(s_gw, e + 1)
                        gather(e + 1, 1 - i)
                        pool.tensor_copy(sst[:, i, :], sidx[:, bass.ds(e * NSL, NSL)]).then_inc(s_ssg, 1)
                        pool.wait_ge(s_ssg, e + 1)
                        stand(pool, s_past2)
                        for c in range(NSL):
                            pool.wait_ge(s_ye, e * NSL + c + 3)
                            stand(pool, s_past2)
                            pool.indirect_dma_start(out=out_rows, in_=ys[i][c][:, :],
                                                    out_offset=bass.IndirectOffsetOnAxis(ap=sst[:, i, c:c + 1], axis=0),
                                                    in_offset=None, bounds_check=NTOK - 1, oob_is_err=False,
                                                    compute_op=ALU.add).then_inc(s_add, 16)
                        pool.wait_ge(s_add, e * NSL * 16 + NSL * 16)
                        pool.sem_inc(s_yf, 1)

            @block.scalar
            def _(act):
                for c in range(2):
                    act.sem_inc(s_ye, 1)

                def silu(e, m):
                    act.wait_ge(s_a, e * UN + m + 1)
                    act.wait_ge(s_h, e * UN + m + 1)
                    act.activation(sa[:, m % 2, :], hp[:, m % 2, 0, :], ACT.Silu).then_inc(s_si, 1)

                def scale(e, i, c):
                    act.wait_ge(s_y, e * NSL + c + 1)
                    if c == 0:
                        act.wait_ge(s_gw, e + 1)
                        act.wait_ge(s_yf, e + 1)
                    act.activation(ys[i][c][:, :], yp[:, c % 2, 0:D], ACT.Copy,
                                   scale=gw[:, i, c:c + 1]).then_inc(s_ye, 1)

                with act.Fori(0, NE // 2) as pair:
                    e2 = pair * 2
                    for i in range(2):
                        e = e2 + i
                        for kind, k in ORDER:
                            if kind == "h":
                                silu(e, k)
                            elif kind == "y":
                                scale(e, i, k)

            @block.tensor
            def _(pe):
                def table():
                    pe_oh = onehot[:, :, :, :].rearrange("p k t e -> p k (t e)")
                    for k in range(2):
                        pe.matmul(hp[:, 0, 0, 0:NTT * NE], tri[:, :], pe_oh[:, k, :], start=(k == 0), stop=(k == 1))
                    for k in range(2):
                        ins = pe.matmul(hp[:, 0, 1, 0:NTT * NE], ones_b[:, :], pe_oh[:, k, :],
                                        start=(k == 0), stop=(k == 1))
                    ins.then_inc(s_cum, 1)
                    for n in range(NPAIR):
                        if n % CH == 0:
                            pe.wait_ge(s_ab, n // CH + 1)
                        ins = pe.matmul(tp[:, 0, 0:2 * COLS], A[:, n, :],
                                        Bt[:, n, :, :].rearrange("p a c -> p (a c)"),
                                        start=(n == 0), stop=(n == NPAIR - 1))
                    ins.then_inc(s_tab, 1)

                def turn(e, i, k):
                    h, c = k // ND, k % ND
                    pe.wait_ge(s_td, e * NTI + k)
                    for j in range(MM // P):
                        ins = pe.transpose(tp[:, k % 2, j * P:(j + 1) * P],
                                           xg[i][h * (MM // P) + j][:, c * P:(c + 1) * P], ident[:, :])
                    ins.then_inc(s_t, 1)

                def hidden(e, i, m):
                    h, f = m // NF, m % NF
                    pe.wait_ge(s_h, e * UN + m + 1)
                    for part in range(2):
                        for c in range(ND):
                            o = part * FF + f * P
                            ins = pe.matmul(hp[:, m % 2, part, :], w1[:, i, c, o:o + P],
                                            xt[:, i, c, h * MM:(h + 1) * MM], start=(c == 0), stop=(c == ND - 1))
                    ins.then_inc(s_a, 1)

                def project(e, i, c):
                    if c % (MM // P) == 0:
                        pe.wait_ge(s_h, e * UN + NF * (c // (MM // P) + 1) + 2)
                    pe.wait_ge(s_ye, e * NSL + c + 1)
                    for f in range(NF):
                        ins = pe.matmul(yp[:, c % 2, 0:D], ht[:, f, c * P:(c + 1) * P], w2[:, i, f, :],
                                        start=(f == 0), stop=(f == NF - 1))
                    ins.then_inc(s_y, 1)

                table()
                pe.wait_ge(s_g[0], NSL * 16)
                pe.wait_ge(s_idx, 1)
                for k in range(NTI):
                    turn(0, 0, k)
                with pe.Fori(0, NE // 2) as pair:
                    e2 = pair * 2
                    for i in range(2):
                        e = e2 + i
                        pe.wait_ge(s_wt[i], e2 * 16 + 32)
                        pe.wait_ge(s_td, e * NTI + NTI + 1)
                        for kind, k in ORDER:
                            if kind == "h":
                                hidden(e, i, k)
                            elif kind == "y":
                                project(e, i, k)
                            else:
                                if k == 0:
                                    pe.wait_ge(s_g[1 - i], e2 * (NSL * 8) + NSL * 16 * (1 + i))
                                turn(e + 1, 1 - i, k)

            @block.vector
            def _(dve):
                steps = [0]

                def link(ins):
                    ins.then_inc(s_d2, 1)
                    steps[0] += 1
                    dve.wait_ge(s_d2, steps[0])

                for c in range(2):
                    dve.sem_inc(s_h, 1)
                dve.sem_inc(s_td, 1)
                dve.wait_ge(s_i, 6)
                dve.wait_ge(s_cum, 1)
                flat = [P, NTT, NE]
                link(dve.tensor_copy(tot[:, :, :], hp[:, 0, 1, 0:NTT * NE].rearrange("p (t e) -> p t e", e=NE)))
                for e in range(NE):
                    ins = dve.tensor_tensor_scan(inc[:, :, e], one[:, :], tot[:, :, e], 0.0, ALU.mult, ALU.add)
                link(ins)
                link(dve.tensor_tensor(inc[:, :, :], inc[:, :, :], tot[:, :, :], ALU.subtract))
                link(dve.tensor_tensor(pos[:, :, :], hp[:, 0, 0, 0:NTT * NE].rearrange("p (t e) -> p t e", e=NE),
                                       inc[:, :, :], ALU.add))
                for k in range(2):
                    ins = dve.tensor_tensor(tmp[:, k, :, :], pos[:, :, :], onehot[:, k, :, :], ALU.mult)
                link(ins)
                link(dve.tensor_reduce(pk[:, :, :], tmp[:, :, :, :], AX.X, ALU.add))
                for k in range(2):
                    ins = dve.tensor_tensor(tmp[:, k, :, :], iota_e[:, :, :], onehot[:, k, :, :], ALU.mult)
                link(ins)
                link(dve.tensor_reduce(ek[:, :, :], tmp[:, :, :, :], AX.X, ALU.add))
                link(dve.tensor_copy(pi[:, :, :], pk[:, :, :]))
                link(dve.tensor_scalar(li[:, :, :], pi[:, :, :], P - 1, None, ALU.bitwise_and))
                link(dve.tensor_copy(af[:, :, :], li[:, :, :]))
                link(dve.tensor_scalar(li[:, :, :], pi[:, :, :], 7, None, ALU.logical_shift_right))
                link(dve.tensor_copy(bf[:, :, :], li[:, :, :]))
                link(dve.scalar_tensor_tensor(bf[:, :, :], ek[:, :, :], float(NSL), bf[:, :, :], ALU.mult, ALU.add))
                link(dve.tensor_scalar(pk[:, :, :], pk[:, :, :], float(CAPACITY), 10000.0, ALU.is_ge, ALU.mult))
                link(dve.tensor_tensor(bf[:, :, :], bf[:, :, :], pk[:, :, :], ALU.add))
                for q in range(NCH):
                    k, t0 = q * CH // NTT, q * CH % NTT
                    w = slice(q * CH, (q + 1) * CH)
                    a_ = af[:, k, t0:t0 + CH].rearrange("p (t o) -> p t o", o=1).broadcast_to([P, CH, P])
                    b_ = bf[:, k, t0:t0 + CH].rearrange("p (t o) -> p t o", o=1).broadcast_to([P, CH, COLS])
                    t_ = iota_t[:, t0:t0 + CH].rearrange("p (t o) -> p t o", o=1).broadcast_to([P, CH, COLS])
                    ia = iota_a[:, :].rearrange("p (o c) -> p o c", o=1)
                    dve.tensor_tensor(A[:, w, :], ia.broadcast_to([P, CH, P]), a_, ALU.is_equal)
                    link(dve.tensor_tensor(Bq[:, :, :], ia[:, :, 0:COLS].broadcast_to([P, CH, COLS]), b_, ALU.is_equal))
                    dve.tensor_tensor(Bt[:, w, 0, :], Bq[:, :, :], t_, ALU.mult)
                    dve.tensor_scalar(Bt[:, w, 1, :], Bq[:, :, :], iota_p[:, 0:1], None, ALU.mult).then_inc(s_ab, 1)
                    dve.wait_ge(s_ab, q + 1)
                dve.wait_ge(s_tab, 1)
                link(dve.tensor_copy(tab[:, :, :], tp[:, 0, 0:2 * COLS].rearrange("p (a c) -> p a c", a=2)))
                dve.tensor_scalar(occ[:, :], tab[:, 0, :], 0.5, float(1 << 20), ALU.is_lt, ALU.mult)
                link(dve.scalar_tensor_tensor(tab[:, 1, :], tab[:, 0, :], float(P), tab[:, 1, :], ALU.mult, ALU.add))
                link(dve.tensor_scalar(tab[:, 1, :], tab[:, 1, :], -float(P), 0.0, ALU.add, ALU.max))
                dve.tensor_copy(gidx[:, 0:COLS], tab[:, 1, :])
                link(dve.tensor_tensor(occ[:, :], occ[:, :], tab[:, 1, :], ALU.add))
                dve.tensor_copy(sidx[:, :], occ[:, :]).then_inc(s_idx, 1)

                def turn(e, i, k):
                    h, c = k // ND, k % ND
                    dve.wait_ge(s_t, e * NTI + k + 1)
                    dve.tensor_copy(xt[:, i, c, h * MM:(h + 1) * MM], tp[:, k % 2, :]).then_inc(s_td, 1)

                def gated(e, i, m):
                    h, f = m // NF, m % NF
                    dve.wait_ge(s_si, e * UN + m + 1)
                    dve.tensor_tensor(ht[:, f, h * MM:(h + 1) * MM], sa[:, m % 2, :], hp[:, m % 2, 1, :],
                                      ALU.mult).then_inc(s_h, 1)

                for k in range(NTI):
                    turn(0, 0, k)
                with dve.Fori(0, NE // 2) as pair:
                    e2 = pair * 2
                    for i in range(2):
                        e = e2 + i
                        dve.wait_ge(s_g[i], e2 * (NSL * 8) + NSL * 16)
                        dve.wait_ge(s_ye, e * NSL + 2)
                        for c in range(NSL):
                            ins = dve.tensor_copy(gw[:, i, c:c + 1], xg[i][c][:, bass.ds(D + e, 1)])
                        ins.then_inc(s_gw, 1)
                        for kind, k in ORDER:
                            if kind == "h":
                                gated(e, i, k)
                            elif kind == "t":
                                turn(e + 1, 1 - i, k)


_INS = ["x", "ctx_512", "L0_xattn_Wq", "L0_xattn_bq", "L0_xattn_Wk", "L0_xattn_bk", "L0_xattn_Wv", "L0_xattn_bv",
        "L0_xattn_Wo", "L0_xattn_bo", "L0_ffn_w_gate", "L0_ffn_c_fc", "L0_ffn_c_proj"]


def kernel(**inputs):
    import numpy as _np
    import concourse.bacc as _bacc
    from concourse import mybir as _mybir
    from concourse.bass_utils import run_bass_kernel_spmd as _run

    nc = _bacc.Bacc("TRN2", target_bir_lowering=False, num_devices=1)
    arrays, args = {}, []
    for name in _INS:
        a = _np.ascontiguousarray(inputs[name])
        arrays[f"in_{name}_dram"] = a
        args.append(nc.dram_tensor(f"in_{name}_dram", a.shape, _mybir.dt.from_np(a.dtype), kind="ExternalInput").ap())
    out = nc.dram_tensor("out_0_dram", inputs["x"].shape, _mybir.dt.float32, kind="ExternalOutput").ap()
    build(nc, *args, out)
    r = _run(nc, [arrays], core_ids=[0])
    return r.results[0]["out_0_dram"]
```

```python
import concourse.bass as bass
from concourse import mybir
from contextlib import ExitStack

P = 128
ALU = mybir.AluOpType
ACT = mybir.ActivationFunctionType
AX = mybir.AxisListType
F32 = mybir.dt.float32
F32R = mybir.dt.float32r
BF16 = mybir.dt.bfloat16
I32 = mybir.dt.int32
U32 = mybir.dt.uint32

EPS = 1e-5
DH = 16
HG = 4
CAPACITY = 1024
SUM_REACH = 1e15
OUT_REACH = 1e30
MM = 512


def r(ap):
    return ap.bitcast(F32R)


HALVES = ((0, 0), (0, 1), (1, 0))


def product(pe, bank, factors):
    terms = [(lhsT, rhs, i, j) for lhsT, rhs in factors for i, j in HALVES]
    for n, (lhsT, rhs, i, j) in enumerate(terms):
        ins = pe.matmul(bank, r(lhsT[:, i]), r(rhs[:, j]), start=(n == 0), stop=(n == len(terms) - 1))
    return ins


def stand(eng, passed):
    eng.sem_inc(passed, 1)


def build(nc, x, ctx, Wq, bq, Wk, bk, Wv, bv, Wo, bo, w_gate, c_fc, c_proj, out):
    B, LQ, D = x.shape
    _, LK, DC = ctx.shape
    H = D // DH
    G = H // HG
    NQ = LQ // P
    ND = D // P
    NT = (LK + P - 1) // P
    LAST = LK - (NT - 1) * P
    NE = w_gate.shape[1]
    NTOK = B * LQ
    NTT = NTOK // P
    FF = c_fc.shape[2] // 2
    NF = FF // P
    XW = D + NE
    SCALE = float(DH) ** -0.5
    STEPS = G * NT
    NB32 = LQ // 32
    NKC = (LK + MM - 1) // MM

    xn2_dram = nc.dram_tensor("xn2_rows", (NTOK, XW), F32, kind="Internal").ap()
    out_rows = out.rearrange("b q d -> (b q) d")

    PREP = ([("xT", c) for c in range(ND)] + [("Q", 0)] + [("cT", k) for k in range(NKC)]
            + [("K", 0, n) for n in range(NKC)] + [("V", k) for k in range(NT)]
            + [item for c in range(1, ND) for item in [("Q", c)] + [("K", c, n) for n in range(NKC)]])
    EPI = [("O", k) for k in range(NQ)] + [("nT", c) for c in range(ND)] + [("lg", t) for t in range(NQ)]
    NP, NEP = len(PREP), len(EPI)
    cT_k, K_k, V_k = PREP.index(("cT", 0)), PREP.index(("K", 0, 0)), PREP.index(("V", 0))
    Q2_k = PREP.index(("Q", ND - 1))
    GC = G // ND
    O_k, nT_k, lg_k = EPI.index(("O", 0)), EPI.index(("nT", 0)), EPI.index(("lg", 0))

    late = ({4 + k: O_k + k for k in range(NQ)} | {10 + c: nT_k + c for c in range(ND)}
            | {10 + ND + t: lg_k + t for t in range(NQ)})
    prep_at, q_half = {}, {}
    u = 10 + ND + NQ
    for k in range(NP):
        if PREP[k][0] == "Q":
            for h in range(ND - 1):
                q_half[u] = (k, h)
                u += 1
        prep_at[u] = k
        u += 1
    assert u <= STEPS
    start_at = {1 + k - V_k - NT: k for k in range(V_k + NT, NP)}
    LN1_STATS, LN1_APPLY, GATE_EXP, GATE_END = 12, 14, 18, 18
    BANK = [(n + 2) % 3 if n < 14 else n % 3 for n in range(2 * STEPS)]
    assert (BANK[-1] + 1) % 3 == BANK[0]
    LINKS = 44

    with ExitStack() as es:
        def sb(name, shape, dt=F32):
            return es.enter_context(nc.sbuf_tensor(name, shape, dt))

        def sem(name):
            return es.enter_context(nc.semaphore(name))

        ident = sb("ident", [P, P])
        tri = sb("tri", [P, P], BF16)
        ones_b = sb("ones_b", [P, P], BF16)
        iota8 = sb("iota8", [P, NQ, NE])
        half = sb("half", [P, NQ])
        redo = sb("redo", [1, 1], I32)
        s_redo = sem("first_pass_judged")
        onehot = sb("onehot", [P, 2, NTT, NE], BF16)

        def attention(shifted):
            again = "_shifted" if shifted else ""
            with ExitStack() as es1:
                def sb1(name, shape, dt=F32):
                    return es1.enter_context(nc.sbuf_tensor(name + again, shape, dt))

                def sem1(name):
                    return es1.enter_context(nc.semaphore(name + again))

                sc = es1.enter_context(nc.psum_tensor("scores" + again, [P, 3, 2 * MM], F32))
                po = es1.enter_context(nc.psum_tensor("attn_out" + again, [P, MM], F32))
                pm = es1.enter_context(nc.psum_tensor("spare" + again, [P, MM], F32))
                BANKS = [pm] + [sc[:, i, j * MM:(j + 1) * MM] for i in range(3) for j in range(2)]
                wq_in = sb1("wq_in", [P, ND, D])
                wk_in = sb1("wk_in", [P, D])
                wv_in = sb1("wv_in", [P, D])
                wo_in = sb1("wo_in", [P, G // 2, D])
                wq = sb1("wq", [P, 2, ND, D])
                wk = sb1("wk", [P, 2, D])
                wv = sb1("wv", [P, 2, D])
                wo = sb1("wo", [P, 2, G // 2, D])
                wg = sb1("wg", [P, ND, NE])
                bqc = sb1("bqc", [P, ND])
                bkc = sb1("bkc", [P, ND])
                bvb = sb1("bvb", [P, D])
                bob = sb1("bob", [P, D])
                x_sb = sb1("x_sb", [P, NQ, D])
                xT = sb1("xT", [P, 2, ND, LQ])
                cT = sb1("cT", [P, 2, LK + 1])
                q_hl = sb1("q_hl", [P, 2, ND, LQ])
                k_hl = sb1("k_hl", [P, 2, ND, LK + 1])
                q_st = sb1("q_st", [P, 2 * HG, LQ])
                k_st = sb1("k_st", [P, HG, LK + 1])
                v_raw = sb1("v_raw", [P, NT, D])
                c_sb = v_raw[:, 0:(NT * DC + D - 1) // D, :].rearrange("p t d -> p (t d)")[:, 0:NT * DC].rearrange(
                    "p (t d) -> p t d", d=DC)
                VW = DH + 1
                v_st = sb1("v_st", [P, NT, H * VW + DH])
                pr = sb1("probs", [P, 2, 2, 2 * MM])
                o_t = sb1("o_t", [P, NB32, 32])
                o_n = sb1("o_n", [P, NB32, 32])
                rec = sb1("rec", [P, NB32])
                rok = sb1("rok", [P, NB32])
                at = sb1("attnT", [P, 2, G // 2, LQ])
                x1 = sb1("x1", [P, NQ, D])
                xn2 = sb1("xn2", [P, NQ, XW])
                nT = sb1("nT", [P, ND, LQ])
                st1 = sb1("st1", [P, NQ, 6])
                mv1 = sb1("mv1", [P, NQ, 2])
                rstd1 = sb1("rstd1", [P, NQ])
                st2 = sb1("st2", [P, NQ, 6])
                mv2 = sb1("mv2", [P, NQ, 2])
                rstd2 = sb1("rstd2", [P, NQ])
                lg = sb1("lg", [P, NQ, NE])
                mx = sb1("mx", [P, NQ, NE])
                mi = sb1("mi", [P, NQ, NE], U32)
                mif = sb1("mif", [P, NQ, 2])
                zz = sb1("zz", [P, NQ, NE])
                ez = sb1("ez", [P, NQ, NE])
                gs = sb1("gs", [P, NQ])
                oh = sb1("oh", [P, 2, NQ, NE])
                if shifted:
                    KM = HG * NQ
                    zrow = sb1("zrow", [2, LQ])
                    mxv = sb1("mxv", [P, KM])
                    mrow = sb1("mrow", [KM, 2, P])
                    s_mr = sem1("unshifted_scores_ready")
                    s_md = sem1("maxima_taken")
                    s_ms = sem1("shift_rows_filled")
                    sflat = sc[:, :, :].rearrange("p a b -> p (a b)")
                else:
                    red = sb1("red", [P, 2, B * G])
                    okc = sb1("okc", [P, 1])
                    onec = sb1("onec", [P, 1])

                s_const = sem1("consts_made")
                s_w = sem1("weights_loaded")
                s_w2 = sem1("late_weights_loaded")
                s_ws = sem1("weights_split")
                s_x = sem1("x_loaded")
                s_c = sem1("ctx_loaded")
                s_xr = sem1("residual_loaded")
                s_st = [sem1(f"stacks_filled{g}") for g in range(G)]
                s_sc = sem1("scores_ready")
                s_exp = sem1("probs_ready")
                s_pv = sem1("pv_done")
                s_oc = sem1("attn_out_copied")
                s_prep = sem1("prep_item_ready")
                s_prepd = sem1("prep_item_taken")
                s_epi = sem1("epi_item_ready")
                s_epid = sem1("epi_item_taken")
                s_v = sem1("v_group_placed")
                s_mv1 = sem1("ln1_stats_ready")
                s_r1 = sem1("ln1_rstd_ready")
                s_mv2 = sem1("ln2_stats_ready")
                s_r2 = sem1("ln2_rstd_ready")
                s_bo = sem1("residual_biased")
                s_z = sem1("gate_logits_shifted")
                s_ez = sem1("gate_exp_ready")
                s_n = sem1("ln2_rows_ready")
                s_nx = sem1("routed_rows_ready")
                s_at = sem1("attnT_ready")
                s_xn = sem1("ln1_rows_ready")
                s_x1o = sem1("x1_stored")
                s_xno = sem1("routed_rows_stored")
                s_ok = sem1("verdict_per_partition")
                s_okp = sem1("verdict_summed")
                s_past = sem1("dve_waits_passed")
                s_past_p = sem1("pool_waits_passed")
                s_past_sp = sem1("sp_waits_passed")
                s_dve = sem1("dve_step")

                block = es1.enter_context(nc.Block())

                def program(engine):
                    def declare(steps):
                        @engine
                        def _(eng):
                            if not shifted:
                                steps(eng)
                            else:
                                eng.wait_ge(s_redo, 1)
                                with eng.If(eng.value_load(redo[0:1, 0:1], min_val=0, max_val=P)):
                                    steps(eng)
                    return declare

                NCONST = 15
                NW = 16 * (ND + 2 + 3)
                NW2 = 16 * (2 + 2 * HG)

                def slot(h):
                    return h % (2 * HG)

                def pair(h):
                    return h // 2 % HG

                STK = 16 * HG * (7 if shifted else 6)

                @program(block.sync)
                def _(sp):
                    sp.dma_start(x_sb[:, :, :], x[0].rearrange("(t p) d -> p t d", p=P)).then_inc(s_x, 16)
                    sp.dma_start(c_sb[:, 0:NT - 1, :],
                                 ctx[0, 0:(NT - 1) * P].rearrange("(t p) d -> p t d", p=P)).then_inc(s_c, 16)
                    sp.dma_start(c_sb[0:LAST, NT - 1, :], ctx[0, (NT - 1) * P:LK]).then_inc(s_c, 16)
                    for c in range(ND):
                        sp.dma_start(wq_in[:, c, :], Wq[c * P:(c + 1) * P, :]).then_inc(s_w, 16)
                    sp.dma_start(wk_in[:, :], Wk).then_inc(s_w, 16)
                    with nc.allow_non_contiguous_dma(reason="bias columns, once"):
                        sp.dma_start(bqc[:, :], bq.rearrange("(c p) -> p c", p=P)).then_inc(s_w, 16)
                        sp.dma_start(bkc[:, :], bk.rearrange("(c p) -> p c", p=P)).then_inc(s_w, 16)
                    sp.dma_start(wv_in[:, :], Wv).then_inc(s_w, 16)
                    sp.dma_start(bvb[:, :], bv.rearrange("(a n) -> a n", a=1).broadcast_to([P, D])).then_inc(s_w, 16)

                    def late_weights():
                        with nc.allow_non_contiguous_dma(reason="gate weights, once"):
                            sp.dma_start(wg[:, :, :], w_gate.rearrange("(c p) e -> p c e", p=P)).then_inc(s_w2, 16)
                        sp.dma_start(bob[:, :], bo.rearrange("(a n) -> a n", a=1).broadcast_to([P, D])).then_inc(s_w2, 16)
                        wo_v = Wo.rearrange("(p i h d) n -> h i d p n", i=2, h=HG, d=DH)
                        for h in range(HG):
                            for i in range(2):
                                row = 32 * h + DH * i
                                sp.dma_start(wo_in[row:row + DH, :, :], wo_v[h, i]).then_inc(s_w2, 16)

                    def stacks(b, g):
                        sp.wait_ge(s_prepd, b * NP + (cT_k if g < GC else Q2_k + 1))
                        stand(sp, s_past_sp)
                        if g >= 2:
                            sp.wait_ge(s_sc, b * 2 * STEPS + 2 * NT * (g - 1))
                        elif not (isinstance(b, int) and b == 0):
                            sp.wait_ge(s_sc, b * 2 * STEPS - 2 * STEPS + 2 * NT * (G + g - 1))
                        heads = [(h, h * DH // P, h * DH % P, 64 * (h % 2)) for h in range(HG * g, HG * g + HG)]
                        for h, c, row, at0 in heads:
                            for k, part in enumerate((0, 1, 0)):
                                sp.dma_start(q_st[at0 + DH * k:at0 + DH * (k + 1), slot(h), :],
                                             q_hl[row:row + DH, part, c, :]).then_inc(s_st[g], 16)
                            if shifted:
                                sp.dma_start(q_st[at0 + 3 * DH:at0 + 3 * DH + 2, slot(h), :], zrow[:, :]).then_inc(s_st[g], 16)
                        sp.wait_ge(s_prepd, b * NP + (V_k if g < GC else NP))
                        for h, c, row, at0 in heads:
                            for k, part in enumerate((0, 0, 1)):
                                sp.dma_start(k_st[at0 + DH * k:at0 + DH * (k + 1), pair(h), :],
                                             k_hl[row:row + DH, part, c, :]).then_inc(s_st[g], 16)

                    sp.wait_ge(s_const, NCONST)
                    stacks(0, 0)
                    late_weights()
                    stacks(0, 1)

                    def store_x1(b):
                        rows = out_rows[bass.ds(b * LQ, LQ), :].rearrange("(t p) d -> p t d", p=P)
                        sp.wait_ge(s_epid, b * NEP + nT_k)
                        sp.dma_start(rows, x1[:, :, :]).then_inc(s_x1o, 16)

                    def store_rows(b):
                        rows = xn2_dram[bass.ds(b * LQ, LQ), :].rearrange("(t p) d -> p t d", p=P)
                        sp.wait_ge(s_nx, b + 1)
                        sp.dma_start(rows, xn2[:, :, :]).then_inc(s_xno, 16)

                    def body(b, first, final):
                        if not final:
                            sp.wait_ge(s_prep, b * NP + ND)
                            sp.dma_start(x_sb[:, :, :],
                                         x[bass.ds(b + 1, 1)].rearrange("o (t p) d -> p (o t) d", p=P)).then_inc(s_x, 16)
                        if not first:
                            stacks(b, 1)
                        if not final:
                            sp.wait_ge(s_v, b * G + G)
                            sp.dma_start(c_sb[:, 0:NT - 1, :],
                                         ctx[bass.ds(b + 1, 1), 0:(NT - 1) * P].rearrange("o (t p) d -> p (o t) d", p=P)).then_inc(s_c, 16)
                            sp.dma_start(c_sb[0:LAST, NT - 1, :],
                                         ctx[bass.ds(b + 1, 1), (NT - 1) * P:LK].rearrange("o p d -> p (o d)")).then_inc(s_c, 16)
                        if not first:
                            store_x1(b - 1)
                        stacks(b, 2)
                        if not first:
                            store_rows(b - 1)
                            sp.wait_ge(s_x1o, 16 * b)
                            sp.wait_ge(s_xno, 16 * b)
                        sp.dma_start(x1[:, :, :], x[bass.ds(b, 1)].rearrange("o (t p) d -> p (o t) d", p=P)).then_inc(s_xr, 16)
                        stacks(b, 3)
                        if not final:
                            stacks(b + 1, 0)

                    body(0, True, False)
                    with sp.Fori(1, B - 1) as b:
                        body(b, False, False)
                    body(B - 1, False, True)
                    store_x1(B - 1)
                    store_rows(B - 1)
                    sp.wait_ge(s_x1o, 16 * B)
                    sp.wait_ge(s_xno, 16 * B)

                @program(block.gpsimd)
                def _(pool):
                    pool.memset(ident[:, :], 0.0).then_inc(s_const, 1)
                    pool.memset(tri[:, :], 1.0).then_inc(s_const, 1)
                    pool.memset(ones_b[:, :], 1.0).then_inc(s_const, 1)
                    pool.memset(half[:, :], -0.5).then_inc(s_const, 1)
                    pool.memset(v_raw[:, NT - 1, :], 0.0).then_inc(s_const, 1)
                    pool.memset(k_hl[:, :, :, LK:LK + 1], 0.0).then_inc(s_const, 1)
                    pool.memset(cT[:, :, LK:LK + 1], 0.0).then_inc(s_const, 1)
                    heads = v_st[:, :, 0:H * VW].rearrange("p t (h c) -> p t h c", h=H)
                    pool.memset(heads[:, :, :, DH:VW], 1.0).then_inc(s_const, 1)
                    pool.memset(v_st[:, :, H * VW:], 1.0).then_inc(s_const, 1)
                    pool.iota(iota8[:, :, :], [[0, NQ], [1, NE]], base=0, channel_multiplier=0,
                              allow_small_or_imprecise_dtypes=True).then_inc(s_const, 1)
                    pool.wait_ge(s_const, 11)
                    pool.affine_select(out=ident[:, :], in_=ident[:, :], compare_op=ALU.not_equal, fill=1.0,
                                       base=0, pattern=[[-1, P]], channel_multiplier=1).then_inc(s_const, 1)
                    pool.affine_select(out=tri[:, :], in_=tri[:, :], compare_op=ALU.is_gt, fill=0.0,
                                       base=0, pattern=[[1, P]], channel_multiplier=-1).then_inc(s_const, 1)
                    pool.memset(q_st[:, :, :], 0.0).then_inc(s_const, 1)
                    if shifted:
                        pool.memset(zrow[:, :], 0.0).then_inc(s_const, 1)
                    else:
                        pool.memset(onec[:, :], 1.0).then_inc(s_const, 1)

                    def ln1(b):
                        pool.wait_ge(s_mv1, b + 1)
                        pool.tensor_tensor(rstd1[:, :], mv1[:, :, 1], half[:, :], ALU.pow).then_inc(s_r1, 1)

                    def place(b, g):
                        if not (isinstance(b, int) and b == 0):
                            pool.wait_ge(s_pv, b * STEPS - STEPS + NT * (g + 1))
                        stand(pool, s_past_p)
                        w = slice(HG * g * VW, HG * (g + 1) * VW)
                        dst = v_st[:, :, w].rearrange("p t (h c) -> p t h c", h=HG)[:, :, :, 0:DH]
                        src = v_raw[:, :, HG * g * DH:HG * (g + 1) * DH].rearrange("p t (h c) -> p t h c", h=HG)
                        for t in range(NT):
                            ins = pool.tensor_copy(dst[:, t], src[:, t])
                        ins.then_inc(s_v, 1)

                    def ln2(b):
                        pool.wait_ge(s_xr, 16 * b + 16)
                        for t in range(NQ):
                            ins = pool.tensor_tensor(x1[:, t, :], x1[:, t, :], bob[:, :], ALU.add)
                        ins.then_inc(s_bo, 1)
                        pool.wait_ge(s_mv2, b + 1)
                        pool.tensor_tensor(rstd2[:, :], mv2[:, :, 1], half[:, :], ALU.pow).then_inc(s_r2, 1)

                    pool.wait_ge(s_const, NCONST)
                    ln1(0)
                    pool.wait_ge(s_prepd, V_k + NT)
                    for g in range(G):
                        place(0, g)

                    def body(b, first, final):
                        if not first:
                            ln2(b - 1)
                        if not final:
                            ln1(b + 1)
                            pool.wait_ge(s_prepd, (b + 1) * NP + V_k + NT)
                            for g in range(G):
                                place(b + 1, g)

                    pool.wait_ge(s_w2, NW2)
                    body(0, True, False)
                    with pool.Fori(1, B - 1) as b:
                        body(b, False, False)
                    body(B - 1, False, True)
                    ln2(B - 1)

                @program(block.scalar)
                def _(act):
                    def body(b, first):
                        for n in range(2 * STEPS):
                            u, j = n // 2, n % 2
                            if shifted and n % (2 * NT) == 0:
                                shift_rows(b, u // NT)
                            rows = P if u % NT < NT - 1 else LAST
                            act.wait_ge(s_sc, b * 2 * STEPS + n + 1)
                            if not (first and u < 2):
                                act.wait_ge(s_pv, b * STEPS + u - 1)
                            act.activation(pr[0:rows, u % 2, j, :], sc[0:rows, BANK[n], :], ACT.Exp,
                                           scale=SCALE).then_inc(s_exp, 1)
                            if n == 2 * GATE_EXP and not first:
                                gate(b - 1)

                    def shift_rows(b, g):
                        act.wait_ge(s_md, (b * G + g + 1) * (KM + 1))
                        for k in range(KM):
                            h = HG * g + k // NQ
                            row, cols = 64 * (h % 2) + 3 * DH, slice(k % NQ * P, (k % NQ + 1) * P)
                            for part in range(2):
                                act.dma_start(q_st[row + part:row + part + 1, slot(h), cols],
                                              mrow[k:k + 1, part, :]).then_inc(s_ms, 16)

                    def gate(b):
                        act.wait_ge(s_z, b + 1)
                        act.activation(ez[:, :, :], zz[:, :, :], ACT.Exp).then_inc(s_ez, 1)

                    body(0, True)
                    with act.Fori(1, B) as b:
                        body(b, False)
                    gate(B - 1)

                @program(block.tensor)
                def _(pe):
                    def prep(b, k, bank=pm):
                        project_q(b, k, range(ND), bank) if PREP[k][0] == "Q" else prep_other(b, k, bank)

                    def project_q(b, k, chunks, bank=pm):
                        c = PREP[k][1]
                        for k2 in chunks:
                            for i, j in HALVES:
                                ins = pe.matmul(bank[:, 0:LQ], r(wq[:, i, k2, c * P:(c + 1) * P]), r(xT[:, j, k2, :]),
                                                start=(k2 == 0 and i + j == 0),
                                                stop=(k2 == ND - 1 and (i, j) == HALVES[-1]))
                        if k2 == ND - 1:
                            ins.then_inc(s_prep, 1)

                    def prep_other(b, k, bank):
                        kind, *arg = PREP[k]
                        if kind == "xT":
                            c, = arg
                            if c == 0:
                                pe.wait_ge(s_xn, b + 1)
                            for t in range(NQ):
                                ins = pe.transpose(bank[:, t * P:(t + 1) * P], x_sb[:, t, c * P:(c + 1) * P], ident[:, :])
                        elif kind == "cT":
                            n, = arg
                            if n == 0:
                                pe.wait_ge(s_c, b * 32 + 32)
                            for t in range(4 * n, min(4 * n + 4, NT)):
                                w = P if t < NT - 1 else LAST
                                ins = pe.transpose(bank[:, (t - 4 * n) * P:(t - 4 * n) * P + w], c_sb[0:w, t, :],
                                                   ident[0:w, 0:w])
                        elif kind == "K":
                            c, n = arg
                            w = min(MM, LK + LK % 2 - n * MM)
                            ins = product(pe, bank[:, 0:w], [(wk[:, :, c * P:(c + 1) * P], cT[:, :, n * MM:n * MM + w])])
                        else:
                            n, = arg
                            w = P if n < NT - 1 else LAST
                            ins = product(pe, bank[0:w, 0:D], [(cT[:, :, n * P:n * P + w], wv[:, :, :])])
                        ins.then_inc(s_prep, 1)

                    def epi(b, k, bank=pm):
                        kind, *arg = EPI[k]
                        if kind == "O":
                            n, = arg
                            if n == 0:
                                pe.wait_ge(s_ws, 4)
                                pe.wait_ge(s_at, b * (G // 2) + G // 2)
                            ins = product(pe, bank[:, 0:D], [(at[:, :, p2, n * P:(n + 1) * P], wo[:, :, p2, :])
                                                       for p2 in range(G // 2)])
                        elif kind == "nT":
                            c, = arg
                            if c == 0:
                                pe.wait_ge(s_n, b + 1)
                            for t in range(NQ):
                                ins = pe.transpose(bank[:, t * P:(t + 1) * P], xn2[:, t, c * P:(c + 1) * P], ident[:, :])
                        else:
                            t, = arg
                            for c in range(ND):
                                ins = pe.matmul(bank[:, 0:NE], nT[:, c, t * P:(t + 1) * P], wg[:, c, :],
                                                start=(c == 0), stop=(c == ND - 1))
                        ins.then_inc(s_epi, 1)

                    def pv(b, u, first):
                        g, t = u // NT, u % NT
                        rows = P if t < NT - 1 else LAST
                        pe.wait_ge(s_exp, b * 2 * STEPS + 2 * u + 2)
                        if t == 0:
                            pe.wait_ge(s_v, b * G + min(g + 2, G))
                            if not (first and g == 0):
                                pe.wait_ge(s_oc, b * G + g)
                        for h in range(HG):
                            c = (HG * g + h) * VW
                            ins = pe.matmul(po[32 * h:32 * h + 32, 0:LQ], v_st[0:rows, t, c:c + 32],
                                            pr[0:rows, u % 2, h // 2, (h % 2) * LQ:(h % 2 + 1) * LQ],
                                            start=(t == 0), stop=(t == NT - 1), tile_position=(0, 32 * h))
                        ins.then_inc(s_pv, 1)

                    def maxima(b, g, u, first):
                        if u > 0 or not first:
                            pe.wait_ge(s_exp, b * 2 * STEPS + 2 * u)
                        done = (b * G + g) * (KM + 1)
                        for k in range(KM):
                            h = HG * g + k // NQ
                            if k > 0:
                                pe.wait_ge(s_md, done + k)
                            for n in range(NKC):
                                w = min(MM, LK + LK % 2 - n * MM)
                                ins = pe.matmul(sflat[:, n * MM:n * MM + w],
                                                r(q_st[:, slot(h), k % NQ * P:(k % NQ + 1) * P]),
                                                r(k_st[:, pair(h), n * MM:n * MM + w]), start=True, stop=True)
                            ins.then_inc(s_mr, 1)
                        pe.wait_ge(s_md, done + KM)
                        pe.transpose(sflat[0:KM, 5 * MM:5 * MM + P], mxv[:, :], ident[:, :]).then_inc(s_mr, 1)
                        pe.wait_ge(s_ms, (b * G + g + 1) * KM * 2 * 16)
                        pe.wait_ge(s_md, done + KM + 1)

                    def body(b, first, final):
                        for u in range(STEPS):
                            g, t = u // NT, u % NT
                            if t == 0:
                                pe.wait_ge(s_st[g], b * STK + STK)
                                if shifted:
                                    maxima(b, g, u, first)
                            rows = P if t < NT - 1 else LAST
                            for j in range(2):
                                n = 2 * u + j
                                before = [m for m in range(n) if BANK[m] == BANK[n]]
                                if before:
                                    pe.wait_ge(s_exp, b * 2 * STEPS + before[-1] + 1)
                                elif not first:
                                    before = max(m for m in range(2 * STEPS) if BANK[m] == BANK[n])
                                    pe.wait_ge(s_exp, b * 2 * STEPS - 2 * STEPS + before + 1)
                                for h in (HG * g + 2 * j, HG * g + 2 * j + 1):
                                    ins = pe.matmul(sc[0:rows, BANK[n], (h % 2) * MM:(h % 2) * MM + LQ],
                                                    r(k_st[:, pair(h), t * P:t * P + rows]), r(q_st[:, slot(h), :]),
                                                    start=True, stop=True)
                                ins.then_inc(s_sc, 1)
                            if u > 0:
                                pv(b, u - 1, first)
                            elif not first:
                                pv(b - 1, STEPS - 1, False)
                            if u in late and not first:
                                if late[u] == 0:
                                    pe.wait_ge(s_prepd, b * NP + NP)
                                else:
                                    pe.wait_ge(s_epid, (b - 1) * NEP + late[u])
                                epi(b - 1, late[u])
                            if first and u in start_at:
                                pe.wait_ge(s_prepd, start_at[u])
                                prep(0, start_at[u])
                            if u in prep_at and not final:
                                k = prep_at[u]
                                if k == 0 and not first:
                                    pe.wait_ge(s_epid, b * NEP)
                                pe.wait_ge(s_prepd, (b + 1) * NP + k)
                                if PREP[k][0] == "Q":
                                    project_q(b + 1, k, range(ND - 1, ND))
                                else:
                                    prep(b + 1, k)
                            if u in q_half and not final:
                                k, h = q_half[u]
                                pe.wait_ge(s_prepd, (b + 1) * NP + k)
                                project_q(b + 1, k, range(h, h + 1))

                    pe.wait_ge(s_const, NCONST)
                    pe.wait_ge(s_w, NW)
                    pe.wait_ge(s_ws, 3)
                    for k in range(V_k + NT):
                        kind, *arg = PREP[k]
                        needs = {"xT": 0, "Q": ND, "cT": 0, "K": cT_k + arg[-1] + 1,
                                 "V": cT_k + arg[-1] * P // MM + 1}[kind]
                        needs = max(needs, k + 1 - len(BANKS))
                        if needs > 0:
                            pe.wait_ge(s_prepd, needs)
                        prep(0, k, BANKS[k % len(BANKS)])
                    pe.wait_ge(s_prepd, V_k + NT)
                    body(0, True, False)
                    with pe.Fori(1, B - 1) as b:
                        body(b, False, False)
                    body(B - 1, False, True)
                    pv(B - 1, STEPS - 1, False)
                    for k in range(NEP):
                        needs = max({"O": 0, "nT": 0, "lg": lg_k}[EPI[k][0]], k + 1 - len(BANKS))
                        pe.wait_ge(s_epid, (B - 1) * NEP + needs)
                        epi(B - 1, k, BANKS[k % len(BANKS)])
                    if not shifted:
                        pe.wait_ge(s_epid, (B - 1) * NEP + NEP)
                        pe.wait_ge(s_ok, 1)
                        pe.matmul(pm[0:1, 0:1], okc[:, 0:1], onec[:, :], start=True, stop=True).then_inc(s_okp, 1)

                @program(block.vector)
                def _(dve):
                    chained = [0]

                    counted = [0]
                    links = LINKS + (G if shifted else 3 * G + 2)

                    def link(ins):
                        ins.then_inc(s_dve, 1)
                        chained[0] = chained[0] + 1
                        counted[0] += 1
                        dve.wait_ge(s_dve, chained[0])

                    def stats(src, t, st):
                        return dve.bn_stats(st[:, t, :], src[:, t, :])

                    def moments(st, mv, signal):
                        stand(dve, s_past)
                        for t in range(NQ):
                            ins = dve.bn_aggr(mv[:, t, :], st[:, t, :])
                        link(ins)
                        dve.tensor_scalar(mv[:, :, 1], mv[:, :, 1], EPS, None, ALU.add).then_inc(signal, 1)

                    def ln1_stats(b):
                        dve.wait_ge(s_x, b * 16 + 16)
                        for t in range(NQ):
                            ins = stats(x_sb, t, st1)
                        link(ins)
                        moments(st1, mv1, s_mv1)

                    def ln1_apply(b):
                        dve.wait_ge(s_mv1, b + 1)
                        dve.wait_ge(s_r1, b + 1)
                        for t in range(NQ):
                            ins = dve.tensor_scalar(x_sb[:, t, :], x_sb[:, t, :], mv1[:, t, 0:1], rstd1[:, t:t + 1],
                                                    ALU.subtract, ALU.mult)
                        ins.then_inc(s_xn, 1)

                    def split(bank, bias, hi, lo):
                        link(dve.tensor_scalar(r(hi), bank, bias, None, ALU.add))
                        dve.scalar_tensor_tensor(r(lo), bank, bias, hi, ALU.add, ALU.subtract).then_inc(s_prepd, 1)

                    def in_halves(whole, hi, lo, signal):
                        link(dve.tensor_copy(r(hi), whole))
                        dve.tensor_tensor(r(lo), whole, hi, ALU.subtract).then_inc(signal, 1)

                    def prep(b, k, bank=pm):
                        kind, *arg = PREP[k]
                        dve.wait_ge(s_prep, b * NP + k + 1)
                        if kind == "xT":
                            in_halves(bank[:, 0:LQ], xT[:, 0, arg[0], :], xT[:, 1, arg[0], :], s_prepd)
                        elif kind == "Q":
                            c, = arg
                            if not (isinstance(b, int) and b == 0):
                                for g in range(GC * c, GC * (c + 1)):
                                    dve.wait_ge(s_st[g], b * STK)
                            split(bank[:, 0:LQ], bqc[:, c:c + 1], q_hl[:, 0, c, :], q_hl[:, 1, c, :])
                        elif kind == "cT":
                            n, = arg
                            w = min(MM, LK - n * MM)
                            in_halves(bank[:, 0:w], cT[:, 0, n * MM:n * MM + w], cT[:, 1, n * MM:n * MM + w], s_prepd)
                        elif kind == "K":
                            c, n = arg
                            w = min(MM, LK - n * MM)
                            at0 = slice(n * MM, n * MM + w)
                            split(bank[:, 0:w], bkc[:, c:c + 1], k_hl[:, 0, c, at0], k_hl[:, 1, c, at0])
                        else:
                            n, = arg
                            if n == 0 and not (isinstance(b, int) and b == 0):
                                dve.wait_ge(s_v, b * G)
                            w = P if n < NT - 1 else LAST
                            dve.tensor_tensor(v_raw[0:w, n, :], bank[0:w, 0:D], bvb[0:w, :], ALU.add).then_inc(s_prepd, 1)

                    def leave(b, g):
                        dve.wait_ge(s_pv, b * STEPS + NT * (g + 1))
                        dve.transpose(o_t[:, :, :].rearrange("p a c -> p (a c)"), po[:, 0:LQ]).then_inc(s_oc, 1)

                    def divide(b, g):
                        dve.wait_ge(s_oc, b * G + g + 1)
                        link(dve.reciprocal(rec[:, :], o_t[:, :, DH]))
                        i = g % 2
                        link(dve.tensor_tensor(o_n[:, :, DH * i:DH * (i + 1)], o_t[:, :, 0:DH],
                                               rec[:, :].rearrange("p (a o) -> p a o", o=1).broadcast_to([P, NB32, DH]),
                                               ALU.mult))

                    def turn_back(b, g):
                        if g % 2 == 1:
                            turned = o_t[:, :, :].rearrange("p a c -> p (a c)")
                            link(dve.transpose(turned, o_n[:, :, :].rearrange("p a c -> p (a c)")))
                            in_halves(turned, at[:, 0, g // 2, :], at[:, 1, g // 2, :], s_at)
                            dve.wait_ge(s_at, b * (G // 2) + g // 2 + 1)

                    def judge(b, g):
                        if not shifted:
                            link(dve.tensor_scalar(rok[:, :], rec[:, :], SUM_REACH, None, ALU.is_lt))
                            link(dve.scalar_tensor_tensor(rok[:, :], rec[:, :], 1.0 / SUM_REACH, rok[:, :],
                                                          ALU.is_gt, ALU.mult))
                            link(dve.tensor_reduce(red[:, 0, bass.ds(b * G + g, 1)], rok[:, :], AX.X, ALU.min,
                                                   negate=True))

                    def finite(b):
                        link(dve.tensor_scalar(rok[:, 0:NQ], mv2[:, :, 1], OUT_REACH, None, ALU.is_lt))
                        link(dve.tensor_reduce(red[:, 1, bass.ds(b * G, 1)], rok[:, 0:NQ], AX.X, ALU.min, negate=True))

                    def verdict():
                        link(dve.tensor_reduce(okc[:, 0:1], red[:, :, :], AX.XY, ALU.max))
                        dve.tensor_scalar(okc[:, 0:1], okc[:, 0:1], -0.5, None, ALU.is_gt).then_inc(s_ok, 1)
                        dve.wait_ge(s_okp, 1)
                        dve.tensor_copy(redo[0:1, 0:1], pm[0:1, 0:1]).then_inc(s_redo, 1)

                    def maxima(b, g):
                        done = (b * G + g) * (KM + 1)
                        for k in range(KM):
                            dve.wait_ge(s_mr, done + k + 1)
                            dve.tensor_reduce(mxv[:, k:k + 1], sflat[:, 0:LK], AX.X, ALU.max).then_inc(s_md, 1)
                        dve.wait_ge(s_mr, done + KM + 1)
                        bank = sflat[0:KM, 5 * MM:5 * MM + P]
                        link(dve.tensor_scalar(r(mrow[:, 0, :]), bank, -1.0, None, ALU.mult))
                        dve.scalar_tensor_tensor(r(mrow[:, 1, :]), bank, -1.0, mrow[:, 0, :], ALU.mult,
                                                 ALU.subtract).then_inc(s_md, 1)

                    def epi(b, k, bank=pm):
                        kind, *arg = EPI[k]
                        dve.wait_ge(s_epi, b * NEP + k + 1)
                        if kind == "O":
                            n, = arg
                            if n == 0:
                                dve.wait_ge(s_bo, b + 1)
                            dve.tensor_tensor(x1[:, n, :], bank[:, 0:D], x1[:, n, :], ALU.add).then_inc(s_epid, 1)
                            dve.wait_ge(s_epid, b * NEP + k + 1)
                            link(stats(x1, n, st2))
                            if n == NQ - 1:
                                moments(st2, mv2, s_mv2)
                        elif kind == "nT":
                            dve.tensor_copy(nT[:, arg[0], :], bank[:, 0:LQ]).then_inc(s_epid, 1)
                        else:
                            t, = arg
                            dve.tensor_copy(lg[:, t, :], bank[:, 0:NE]).then_inc(s_epid, 1)
                            if t == NQ - 1:
                                gate(b, k)

                    def ln2_apply(b):
                        dve.wait_ge(s_mv2, b + 1)
                        if not shifted:
                            finite(b)
                        dve.wait_ge(s_r2, b + 1)
                        for t in range(NQ):
                            ins = dve.tensor_scalar(xn2[:, t, 0:D], x1[:, t, :], mv2[:, t, 0:1], rstd2[:, t:t + 1],
                                                    ALU.subtract, ALU.mult)
                        ins.then_inc(s_n, 1)

                    def gate(b, k):
                        dve.wait_ge(s_epid, b * NEP + k + 1)
                        stand(dve, s_past)
                        for t in range(NQ):
                            ins = dve.max(mx[:, t, :], lg[:, t, :])
                        link(ins)
                        dve.tensor_tensor(zz[:, :, :], lg[:, :, :], mx[:, :, 0:1].broadcast_to([P, NQ, NE]),
                                          ALU.subtract).then_inc(s_z, 1)
                        for t in range(NQ):
                            ins = dve.max_index(mi[:, t, :], mx[:, t, :], lg[:, t, :])
                        link(ins)
                        link(dve.tensor_copy(mif[:, :, :], mi[:, :, 0:2]))
                        for k2 in range(2):
                            ins = dve.tensor_tensor(oh[:, k2, :, :], iota8[:, :, :],
                                                    mif[:, :, k2:k2 + 1].broadcast_to([P, NQ, NE]), ALU.is_equal)
                        link(ins)

                    def gates(b):
                        dve.wait_ge(s_ez, b + 1)
                        link(dve.tensor_reduce(gs[:, :], ez[:, :, :], AX.X, ALU.add))
                        link(dve.reciprocal(gs[:, :], gs[:, :]))
                        link(dve.tensor_tensor(ez[:, :, :], ez[:, :, :],
                                               gs[:, :].rearrange("p (t o) -> p t o", o=1).broadcast_to([P, NQ, NE]), ALU.mult))
                        link(dve.tensor_tensor(lg[:, :, :], oh[:, 0, :, :], oh[:, 1, :, :], ALU.add))
                        dve.tensor_tensor(xn2[:, :, D:XW], ez[:, :, :], lg[:, :, :], ALU.mult).then_inc(s_nx, 1)
                        link(dve.tensor_copy(onehot[:, :, bass.ds(b * NQ, NQ), :], oh[:, :, :, :]))

                    def body(b, first, final):
                        for u in range(STEPS):
                            if shifted and u % NT == 0:
                                maxima(b, u // NT)
                            group_done = (b, u // NT - 1) if u >= NT else None if first else (b - 1, G - 1)
                            if u % NT == 0 and group_done:
                                leave(*group_done)
                            if u in late and not first:
                                epi(b - 1, late[u])
                            if first and u in start_at:
                                prep(0, start_at[u])
                            if u in prep_at and not final:
                                prep(b + 1, prep_at[u])
                            for step, work in enumerate((divide, turn_back, judge)):
                                if u % NT == 1 + step and group_done:
                                    work(*group_done)
                            if u == 8 and not first:
                                ln2_apply(b - 1)
                            if u == LN1_STATS and not final:
                                ln1_stats(b + 1)
                            if u == GATE_END and not first:
                                gates(b - 1)
                            if u == LN1_APPLY and not final:
                                ln1_apply(b + 1)

                    dve.memset(k_st[:, :, :], 1.0).then_inc(s_const, 1)
                    if not shifted:
                        link(dve.memset(red[:, :, :], -1.0))
                    ln1_stats(0)
                    dve.wait_ge(s_w, NW)
                    in_halves(wq_in[:, :, :], wq[:, 0], wq[:, 1], s_ws)
                    in_halves(wk_in[:, :], wk[:, 0], wk[:, 1], s_ws)
                    in_halves(wv_in[:, :], wv[:, 0], wv[:, 1], s_ws)
                    ln1_apply(0)
                    for k in range(V_k + NT):
                        prep(0, k, BANKS[k % len(BANKS)])
                    dve.wait_ge(s_w2, NW2)
                    in_halves(wo_in[:, :, :], wo[:, 0], wo[:, 1], s_ws)
                    body(0, True, False)
                    start = chained[0]
                    with dve.Fori(1, B - 1) as b:
                        chained[0] = (b - 1) * links + start
                        counted[0] = 0
                        body(b, False, False)
                        assert counted[0] == links, counted[0]
                    chained[0] = (B - 2) * links + start
                    body(B - 1, False, True)
                    leave(B - 1, G - 1)
                    divide(B - 1, G - 1)
                    turn_back(B - 1, G - 1)
                    judge(B - 1, G - 1)
                    for k in range(NEP):
                        epi(B - 1, k, BANKS[k % len(BANKS)])
                        if k == O_k + NQ - 1:
                            ln2_apply(B - 1)
                    gates(B - 1)
                    if not shifted:
                        verdict()

        attention(False)
        attention(True)

        NSL = CAPACITY // P
        NPAIR = 2 * NTT
        CH = min(16, NTT & -NTT)
        NCH = NPAIR // CH
        COLS = NE * NSL
        with ExitStack() as es2:
            def sb2(name, shape, dt=F32):
                return es2.enter_context(nc.sbuf_tensor(name, shape, dt))

            def sem2(name):
                return es2.enter_context(nc.semaphore(name))

            gidx = sb2("gidx", [P, COLS + NSL], I32)
            sidx = sb2("sidx", [P, COLS], I32)
            gst = sb2("gst", [P, 2, NSL], I32)
            sst = sb2("sst", [P, 2, NSL], I32)
            w1_in = sb2("w1_in", [P, 2, ND, 2 * FF])
            w2_in = sb2("w2_in", [P, 2, NF, D])
            xg = [[sb2(f"xg{i}_{c}", [P, XW]) for c in range(NSL)] for i in range(2)]
            gw = sb2("gw", [P, 2, NSL])

            with ExitStack() as es3:
                def sb3(name, shape, dt=F32):
                    return es3.enter_context(nc.sbuf_tensor(name, shape, dt))

                iota_a = sb3("iota_a", [P, P, CH], BF16)
                iota_t = sb3("iota_t", [P, NTT], BF16)
                iota_p = sb3("iota_p", [P, 1])
                iota_e = sb3("iota_e", [P, NTT, NE])
                tot = sb3("tot", [P, NTT, NE])
                inc = sb3("inc", [P, NTT, NE])
                pos = sb3("pos", [P, NTT, NE])
                one = sb3("one", [P, NTT])
                tmp = sb3("tmp", [P, 2, NTT, NE])
                pk = sb3("pk", [P, 2, NTT])
                ek = sb3("ek", [P, 2, NTT])
                pi = sb3("pi", [P, 2, NTT], I32)
                li = sb3("li", [P, 2, NTT], I32)
                bf = sb3("bf", [P, 2, NTT])
                a_b = sb3("a_b", [P, 2, NTT], BF16)
                b_b = sb3("b_b", [P, 2, NTT], BF16)
                A = sb3("A", [P, NCH, P, CH], BF16)
                Bq = sb3("Bq", [P, COLS, CH], BF16)
                Bt = sb3("Bt", [P, NCH, 2, COLS, CH], BF16)
                tab = sb3("tab", [P, 2, COLS])
                occ = sb3("occ", [P, COLS])
            w1 = sb2("w1", [P, 2, 2, ND, 2 * FF])
            w2 = sb2("w2", [P, 2, 2, NF, D])
            xt = sb2("xt", [P, 2, 2, ND, CAPACITY])
            sa = sb2("sa", [P, 2, MM])
            hw = sb2("hw", [P, 2, MM])
            ht = sb2("ht", [P, 2, NF, CAPACITY])
            ys = [[sb2(f"y{i}_{c}", [P, D]) for c in range(NSL)] for i in range(2)]

            hp = es2.enter_context(nc.psum_tensor("h_banks", [P, 2, 2, MM], F32))
            tp = es2.enter_context(nc.psum_tensor("t_banks", [P, 2, MM], F32))
            yp = es2.enter_context(nc.psum_tensor("y_banks", [P, 2, MM], F32))

            s_i = sem2("iotas_made")
            s_cum = sem2("counts_ready")
            s_ab = sem2("onehots_ready")
            s_tab = sem2("table_ready")
            s_idx = sem2("indices_ready")
            s_w12 = sem2("expert_weights_split")
            s_d3 = sem2("dve_step3")
            s_wt = [sem2(f"expert_weights{i}") for i in range(2)]
            s_stg = sem2("gather_indices_staged")
            s_ssg = sem2("scatter_indices_staged")
            s_g = [sem2(f"rows_gathered{i}") for i in range(2)]
            s_g1 = [sem2(f"first_rows_gathered{i}") for i in range(2)]
            s_t = sem2("rows_transposed")
            s_th = sem2("rows_T_high_ready")
            s_wh = sem2("weights_high_ready")
            s_td = sem2("rows_T_copied")
            s_a = sem2("hidden_ready")
            s_si = sem2("silu_ready")
            s_h = sem2("gated_ready")
            s_y = sem2("y_ready")
            s_ye = sem2("y_scaled")
            s_gw = sem2("gates_ready")
            s_yf = sem2("experts_added")
            s_add = sem2("y_added")
            s_d2 = sem2("dve_step2")
            s_past2 = sem2("pool_waits_passed2")
            block = es2.enter_context(nc.Block())

            H2 = CAPACITY // MM
            UN = H2 * NF
            NTI = H2 * ND

            QU = MM // P
            tail = [("y", k) for k in range(QU, NSL)]
            for k in range(2, NTI):
                tail.insert(2 * k - 3, ("t", k))
            ORDER = ([("h", k) for k in range(NF)] + [("w high", 0), ("h", NF), ("w low", 0)]
                     + [("y", k) for k in range(QU - 1)]
                     + [("h", k) for k in range(NF + 1, UN)] + [("y", QU - 1), ("t", 0), ("t", 1)] + tail)

            @block.sync
            def _(sp):
                def load(e, i):
                    sp.dma_start(w1_in[:, i, :, :],
                                 c_fc[bass.ds(e, 1)].rearrange("o (c p) f -> p (o c) f", p=P)).then_inc(s_wt[i], 16)
                    sp.dma_start(w2_in[:, i, :, :],
                                 c_proj[bass.ds(e, 1)].rearrange("o (c p) f -> p (o c) f", p=P)).then_inc(s_wt[i], 16)

                load(0, 0)
                load(1, 1)
                with sp.Fori(0, NE // 2 - 1) as pair:
                    e = pair * 2
                    for i in range(2):
                        sp.wait_ge(s_w12, e + i + 1)
                        load(e + i + 2, i)

            @block.gpsimd
            def _(pool):
                pool.iota(iota_e[:, :, :], [[0, NTT], [1, NE]], base=0, channel_multiplier=0,
                          allow_small_or_imprecise_dtypes=True).then_inc(s_i, 1)
                pool.memset(one[:, :], 1.0).then_inc(s_i, 1)
                pool.iota(iota_a[:, :, :], [[1, P], [0, CH]], base=0, channel_multiplier=0,
                          allow_small_or_imprecise_dtypes=True).then_inc(s_i, 1)
                pool.iota(iota_t[:, :], [[1, NTT]], base=1, channel_multiplier=0,
                          allow_small_or_imprecise_dtypes=True).then_inc(s_i, 1)
                pool.iota(iota_p[:, :], [[0, 1]], base=0, channel_multiplier=1,
                          allow_small_or_imprecise_dtypes=True).then_inc(s_i, 1)
                pool.memset(gidx[:, COLS:], 0).then_inc(s_i, 1)

                def gather(e, i):
                    stand(pool, s_past2)
                    pool.tensor_copy(gst[:, i, :], gidx[:, bass.ds(e * NSL, NSL)]).then_inc(s_stg, 1)
                    pool.wait_ge(s_stg, e + 1)
                    stand(pool, s_past2)
                    for c in range(NSL):
                        pool.indirect_dma_start(out=xg[i][c][:, :], out_offset=None, in_=xn2_dram[:, :],
                                                in_offset=bass.IndirectOffsetOnAxis(ap=gst[:, i, c:c + 1], axis=0),
                                                bounds_check=NTOK - 1,
                                                oob_is_err=False).then_inc(s_g1[i] if c < NSL // 2 else s_g[i], 16)

                def gates(e, i, gathered):
                    for part in (s_g1[i], s_g[i]):
                        pool.wait_ge(part, gathered)
                        stand(pool, s_past2)
                    pool.wait_ge(s_ye, e * NSL + 2)
                    stand(pool, s_past2)
                    for c in range(NSL):
                        ins = pool.tensor_copy(gw[:, i, c:c + 1], xg[i][c][:, bass.ds(D + e, 1)])
                    ins.then_inc(s_gw, 1)

                for c in range(2):
                    pool.sem_inc(s_yf, 1)
                pool.wait_ge(s_idx, 1)
                gather(0, 0)
                with pool.Fori(0, NE // 2) as pair:
                    e2 = pair * 2
                    for i in range(2):
                        e = e2 + i
                        gates(e, i, e2 * (NSL * 4) + NSL * 8)
                        pool.wait_ge(s_t, e * NTI + NTI)
                        pool.wait_ge(s_gw, e + 1)
                        gather(e + 1, 1 - i)
                        pool.tensor_copy(sst[:, i, :], sidx[:, bass.ds(e * NSL, NSL)]).then_inc(s_ssg, 1)
                        pool.wait_ge(s_ssg, e + 1)
                        stand(pool, s_past2)
                        for c in range(NSL):
                            pool.wait_ge(s_ye, e * NSL + c + 3)
                            stand(pool, s_past2)
                            pool.indirect_dma_start(out=out_rows, in_=ys[i][c][:, :],
                                                    out_offset=bass.IndirectOffsetOnAxis(ap=sst[:, i, c:c + 1], axis=0),
                                                    in_offset=None, bounds_check=NTOK - 1, oob_is_err=False,
                                                    compute_op=ALU.add).then_inc(s_add, 16)
                        pool.wait_ge(s_add, e * NSL * 16 + NSL * 16)
                        pool.sem_inc(s_yf, 1)

            @block.scalar
            def _(act):
                for c in range(2):
                    act.sem_inc(s_ye, 1)

                def silu(e, m):
                    act.wait_ge(s_a, e * UN + m + 1)
                    act.wait_ge(s_h, e * UN + m + 1)
                    act.activation(sa[:, m % 2, :], hp[:, m % 2, 0, :], ACT.Silu).then_inc(s_si, 1)

                def scale(e, i, c):
                    act.wait_ge(s_y, e * NSL + c + 1)
                    if c == 0:
                        act.wait_ge(s_gw, e + 1)
                        act.wait_ge(s_yf, e + 1)
                    act.activation(ys[i][c][:, :], yp[:, c % 2, 0:D], ACT.Copy,
                                   scale=gw[:, i, c:c + 1]).then_inc(s_ye, 1)

                def turn(e, i, k):
                    h, c = k // ND, k % ND
                    act.wait_ge(s_t, e * NTI + k + 1)
                    act.activation(r(xt[:, i, 0, c, h * MM:(h + 1) * MM]), tp[:, k % 2, :], ACT.Copy).then_inc(s_th, 1)

                def split_weights(i, loaded):
                    act.wait_ge(s_wt[i], loaded)
                    act.activation(r(w1[:, i, 0]), w1_in[:, i], ACT.Copy).then_inc(s_wh, 1)
                    act.activation(r(w2[:, i, 0]), w2_in[:, i], ACT.Copy).then_inc(s_wh, 1)

                def experts(e2, final):
                    for i in range(2):
                        e = e2 + i
                        for kind, k in ORDER:
                            if kind == "h":
                                silu(e, k)
                            elif kind == "y":
                                scale(e, i, k)
                            elif kind == "t":
                                turn(e + 1, 1 - i, k)
                            elif kind == "w high" and (i == 0 or not final):
                                split_weights(1 - i, e2 * 16 + 32 + 32 * i)

                act.wait_ge(s_idx, 1)
                split_weights(0, 32)
                for k in range(NTI):
                    turn(0, 0, k)
                with act.Fori(0, NE // 2 - 1) as pair:
                    experts(pair * 2, False)
                experts(NE - 2, True)

            @block.tensor
            def _(pe):
                def table():
                    pe_oh = onehot[:, :, :, :].rearrange("p k t e -> p k (t e)")
                    for k in range(2):
                        pe.matmul(hp[:, 0, 0, 0:NTT * NE], tri[:, :], pe_oh[:, k, :], start=(k == 0), stop=(k == 1))
                    for k in range(2):
                        ins = pe.matmul(hp[:, 0, 1, 0:NTT * NE], ones_b[:, :], pe_oh[:, k, :],
                                        start=(k == 0), stop=(k == 1))
                    ins.then_inc(s_cum, 1)
                    for n in range(NPAIR):
                        if n % CH == 0:
                            pe.wait_ge(s_ab, n // CH + 1)
                        ins = pe.matmul(tp[:, 0, 0:2 * COLS], A[:, n // CH, :, n % CH],
                                        Bt[:, n // CH, :, :, n % CH].rearrange("p a c -> p (a c)"),
                                        start=(n == 0), stop=(n == NPAIR - 1))
                    ins.then_inc(s_tab, 1)

                def turn(e, i, k):
                    h, c = k // ND, k % ND
                    pe.wait_ge(s_td, e * NTI + k)
                    for j in range(MM // P):
                        ins = pe.transpose(tp[:, k % 2, j * P:(j + 1) * P],
                                           xg[i][h * (MM // P) + j][:, c * P:(c + 1) * P], ident[:, :])
                    ins.then_inc(s_t, 1)

                def hidden(e, i, m):
                    h, f = m // NF, m % NF
                    if f == 0:
                        pe.wait_ge(s_td, e * NTI + ND * (h + 1) + 1)
                    pe.wait_ge(s_h, e * UN + m + 1)
                    for part in range(2):
                        o = part * FF + f * P
                        ins = product(pe, hp[:, m % 2, part, :], [(w1[:, i, :, c, o:o + P],
                                                                   xt[:, i, :, c, h * MM:(h + 1) * MM]) for c in range(ND)])
                    ins.then_inc(s_a, 1)

                def project(e, i, c):
                    if c % (MM // P) == 0:
                        pe.wait_ge(s_h, e * UN + NF * (c // (MM // P) + 1) + 2)
                    pe.wait_ge(s_ye, e * NSL + c + 1)
                    ins = product(pe, yp[:, c % 2, 0:D], [(ht[:, :, f, c * P:(c + 1) * P], w2[:, i, :, f, :])
                                                          for f in range(NF)])
                    ins.then_inc(s_y, 1)

                table()
                pe.wait_ge(s_idx, 1)
                for k in range(NTI):
                    if k % ND == 0:
                        pe.wait_ge(s_g[0] if k else s_g1[0], NSL * 8)
                    turn(0, 0, k)
                with pe.Fori(0, NE // 2) as pair:
                    e2 = pair * 2
                    for i in range(2):
                        e = e2 + i
                        pe.wait_ge(s_w12, e + 1)
                        for kind, k in ORDER:
                            if kind == "h":
                                hidden(e, i, k)
                            elif kind == "y":
                                project(e, i, k)
                            elif kind == "t":
                                if k == 0:
                                    pe.wait_ge(s_g1[1 - i], e2 * (NSL * 4) + NSL * 8 * (1 + i))
                                if k == ND:
                                    pe.wait_ge(s_g[1 - i], e2 * (NSL * 4) + NSL * 8 * (1 + i))
                                turn(e + 1, 1 - i, k)

            @block.vector
            def _(dve):
                steps = [0]

                def link(ins):
                    ins.then_inc(s_d2, 1)
                    steps[0] += 1
                    dve.wait_ge(s_d2, steps[0])

                for c in range(2):
                    dve.sem_inc(s_h, 1)
                dve.sem_inc(s_td, 1)
                dve.wait_ge(s_i, 2)
                dve.wait_ge(s_cum, 1)
                flat = [P, NTT, NE]
                link(dve.tensor_copy(tot[:, :, :], hp[:, 0, 1, 0:NTT * NE].rearrange("p (t e) -> p t e", e=NE)))
                for e in range(NE):
                    ins = dve.tensor_tensor_scan(inc[:, :, e], one[:, :], tot[:, :, e], 0.0, ALU.mult, ALU.add)
                link(ins)
                link(dve.tensor_tensor(inc[:, :, :], inc[:, :, :], tot[:, :, :], ALU.subtract))
                link(dve.tensor_tensor(pos[:, :, :], hp[:, 0, 0, 0:NTT * NE].rearrange("p (t e) -> p t e", e=NE),
                                       inc[:, :, :], ALU.add))
                for k in range(2):
                    ins = dve.tensor_tensor(tmp[:, k, :, :], pos[:, :, :], onehot[:, k, :, :], ALU.mult)
                link(ins)
                link(dve.tensor_reduce(pk[:, :, :], tmp[:, :, :, :], AX.X, ALU.add))
                for k in range(2):
                    ins = dve.tensor_tensor(tmp[:, k, :, :], iota_e[:, :, :], onehot[:, k, :, :], ALU.mult)
                link(ins)
                link(dve.tensor_reduce(ek[:, :, :], tmp[:, :, :, :], AX.X, ALU.add))
                link(dve.tensor_copy(pi[:, :, :], pk[:, :, :]))
                link(dve.tensor_scalar(li[:, :, :], pi[:, :, :], P - 1, None, ALU.bitwise_and))
                link(dve.tensor_copy(a_b[:, :, :], li[:, :, :]))
                link(dve.tensor_scalar(li[:, :, :], pi[:, :, :], 7, None, ALU.logical_shift_right))
                link(dve.tensor_copy(bf[:, :, :], li[:, :, :]))
                link(dve.scalar_tensor_tensor(bf[:, :, :], ek[:, :, :], float(NSL), bf[:, :, :], ALU.mult, ALU.add))
                link(dve.tensor_scalar(pk[:, :, :], pk[:, :, :], float(CAPACITY), 10000.0, ALU.is_ge, ALU.mult))
                link(dve.tensor_tensor(b_b[:, :, :], bf[:, :, :], pk[:, :, :], ALU.add))
                dve.wait_ge(s_i, 6)
                for q in range(NCH):
                    k, t0 = q * CH // NTT, q * CH % NTT
                    a_ = a_b[:, k, t0:t0 + CH].rearrange("p (o t) -> p o t", o=1).broadcast_to([P, P, CH])
                    b_ = b_b[:, k, t0:t0 + CH].rearrange("p (o t) -> p o t", o=1).broadcast_to([P, COLS, CH])
                    t_ = iota_t[:, t0:t0 + CH].rearrange("p (o t) -> p o t", o=1).broadcast_to([P, COLS, CH])
                    dve.tensor_tensor(A[:, q, :, :], iota_a[:, :, :], a_, ALU.is_equal)
                    link(dve.tensor_tensor(Bq[:, :, :], iota_a[:, 0:COLS, :], b_, ALU.is_equal))
                    dve.tensor_tensor(Bt[:, q, 0, :, :], Bq[:, :, :], t_, ALU.mult)
                    dve.tensor_scalar(Bt[:, q, 1, :, :], Bq[:, :, :], iota_p[:, 0:1], None, ALU.mult).then_inc(s_ab, 1)
                    dve.wait_ge(s_ab, q + 1)
                dve.wait_ge(s_tab, 1)
                link(dve.tensor_copy(tab[:, :, :], tp[:, 0, 0:2 * COLS].rearrange("p (a c) -> p a c", a=2)))
                dve.tensor_scalar(occ[:, :], tab[:, 0, :], 0.5, float(1 << 20), ALU.is_lt, ALU.mult)
                link(dve.scalar_tensor_tensor(tab[:, 1, :], tab[:, 0, :], float(P), tab[:, 1, :], ALU.mult, ALU.add))
                link(dve.tensor_scalar(tab[:, 1, :], tab[:, 1, :], -float(P), 0.0, ALU.add, ALU.max))
                dve.tensor_copy(gidx[:, 0:COLS], tab[:, 1, :])
                link(dve.tensor_tensor(occ[:, :], occ[:, :], tab[:, 1, :], ALU.add))
                dve.tensor_copy(sidx[:, :], occ[:, :]).then_inc(s_idx, 1)

                chain = [0]
                LINKS2 = 2 * UN

                def link3(ins):
                    ins.then_inc(s_d3, 1)
                    chain[0] = chain[0] + 1
                    dve.wait_ge(s_d3, chain[0])

                def turn(e, i, k):
                    h, c = k // ND, k % ND
                    cols = slice(h * MM, (h + 1) * MM)
                    dve.wait_ge(s_th, e * NTI + k + 1)
                    dve.tensor_tensor(r(xt[:, i, 1, c, cols]), tp[:, k % 2, :], xt[:, i, 0, c, cols],
                                      ALU.subtract).then_inc(s_td, 1)

                def gated(e, i, m):
                    h, f = m // NF, m % NF
                    cols = slice(h * MM, (h + 1) * MM)
                    dve.wait_ge(s_si, e * UN + m + 1)
                    link3(dve.tensor_tensor(hw[:, m % 2, :], sa[:, m % 2, :], hp[:, m % 2, 1, :], ALU.mult))
                    link3(dve.tensor_copy(r(ht[:, 0, f, cols]), hw[:, m % 2, :]))
                    dve.tensor_tensor(r(ht[:, 1, f, cols]), hw[:, m % 2, :], ht[:, 0, f, cols],
                                      ALU.subtract).then_inc(s_h, 1)

                def split_weights(e, i):
                    dve.wait_ge(s_wh, e * 2 + 1)
                    dve.tensor_tensor(r(w1[:, i, 1]), w1_in[:, i], w1[:, i, 0], ALU.subtract)
                    dve.wait_ge(s_wh, e * 2 + 2)
                    dve.tensor_tensor(r(w2[:, i, 1]), w2_in[:, i], w2[:, i, 0], ALU.subtract).then_inc(s_w12, 1)

                def experts(e2, final):
                    for i in range(2):
                        e = e2 + i
                        chain[0] = e * LINKS2
                        for kind, k in ORDER:
                            if kind == "h":
                                gated(e, i, k)
                            elif kind == "t":
                                turn(e + 1, 1 - i, k)
                            elif kind == "w low" and (i == 0 or not final):
                                split_weights(e + 1, 1 - i)

                split_weights(0, 0)
                for k in range(NTI):
                    turn(0, 0, k)
                with dve.Fori(0, NE // 2 - 1) as pair:
                    experts(pair * 2, False)
                experts(NE - 2, True)


_INS = ["x", "ctx_512", "L0_xattn_Wq", "L0_xattn_bq", "L0_xattn_Wk", "L0_xattn_bk", "L0_xattn_Wv", "L0_xattn_bv",
        "L0_xattn_Wo", "L0_xattn_bo", "L0_ffn_w_gate", "L0_ffn_c_fc", "L0_ffn_c_proj"]


def kernel(**inputs):
    import numpy as _np
    import concourse.bacc as _bacc
    from concourse import mybir as _mybir
    from concourse.bass_utils import run_bass_kernel_spmd as _run

    nc = _bacc.Bacc("TRN2", target_bir_lowering=False, num_devices=1)
    arrays, args = {}, []
    for name in _INS:
        a = _np.ascontiguousarray(inputs[name])
        arrays[f"in_{name}_dram"] = a
        args.append(nc.dram_tensor(f"in_{name}_dram", a.shape, _mybir.dt.from_np(a.dtype), kind="ExternalInput").ap())
    out = nc.dram_tensor("out_0_dram", inputs["x"].shape, _mybir.dt.float32, kind="ExternalOutput").ap()
    build(nc, *args, out)
    r = _run(nc, [arrays], core_ids=[0])
    return r.results[0]["out_0_dram"]
```
